# Optimizing a Trainium2 kernel written in Bass

```python
import numpy as np
import jax
import jax.numpy as jnp

def _softmax(x, axis=-1):
    return jax.nn.softmax(x, axis=axis)

def _gelu(x):
    return jax.nn.gelu(x, approximate=True)

def _silu(x):
    return jax.nn.silu(x)

def _sigmoid(x):
    return jax.nn.sigmoid(x)

def _layernorm(x, axis=-1, eps=1e-05):
    m = jnp.mean(x, axis=axis, keepdims=True)
    v = jnp.var(x, axis=axis, keepdims=True)
    return (x - m) / jnp.sqrt(v + eps)

def _scatter_add(tgt, idx, src, axis=0):
    return tgt.at[idx].add(src)

def _segment_sum(src, seg, n):
    return jax.ops.segment_sum(src, seg, n)
kernel_name = 'mk_prb_d1_jaxref_r4_01d94d'

def setup_inputs(seed: int=0):
    np.random.seed(seed)
    _w = jnp.asarray

    def _L0_attn_setup():
        import jax, jax.numpy as jnp
        import numpy as np
        B, N, E, H = (2, 512, 256, 8)
        HID = 256
        D = HID // H
        EPS = 1e-08

        def rms_norm(x, scale):
            rms = jnp.linalg.norm(x, axis=-1, keepdims=True) * x.shape[-1] ** (-0.5)
            return scale * (x / (rms + EPS))
        key = jax.random.key(seed)
        ks = jax.random.split(key, 12)
        s = 0.02
        return {'x': jax.random.normal(ks[0], (B, N, E), jnp.float32), 'Wq': jax.random.normal(ks[1], (HID, E), jnp.float32) * s, 'bq': jnp.zeros((HID,), jnp.float32), 'Wk': jax.random.normal(ks[2], (HID, E), jnp.float32) * s, 'bk': jnp.zeros((HID,), jnp.float32), 'Wv': jax.random.normal(ks[3], (HID, E), jnp.float32) * s, 'bv': jnp.zeros((HID,), jnp.float32), 'Wu': jax.random.normal(ks[4], (HID, E), jnp.float32) * s, 'bu': jnp.zeros((HID,), jnp.float32), 'Wo': jax.random.normal(ks[5], (E, HID), jnp.float32) * s, 'bo': jnp.zeros((E,), jnp.float32), 'scale': jnp.ones((HID,), jnp.float32)}
    _L0_attn_in = _L0_attn_setup()

    def _L0_ffn_setup():
        import jax, jax.numpy as jnp
        import numpy as np
        B, T, D, E, H = (8, 512, 256, 8, 64)
        LN_EPS = 1e-05
        key = jax.random.key(seed)
        ks = jax.random.split(key, 4)
        return {'x': jax.random.normal(ks[0], (B, T, D), dtype=jnp.float32), 'Wg': jax.random.normal(ks[1], (E, D), dtype=jnp.float32) * 0.02, 'ln_scale': jnp.ones((E, D), dtype=jnp.float32), 'ln_bias': jnp.zeros((E, D), dtype=jnp.float32), 'W1': jax.random.normal(ks[2], (E, D, H), dtype=jnp.float32) * 0.02, 'b1': jnp.zeros((E, H), dtype=jnp.float32), 'W2': jax.random.normal(ks[3], (E, H, D), dtype=jnp.float32) * 0.02, 'b2': jnp.zeros((E, D), dtype=jnp.float32)}
    _L0_ffn_in = _L0_ffn_setup()
    _d = {'L0_attn_x': _L0_attn_in['x'], 'L0_attn_Wq': _L0_attn_in['Wq'], 'L0_attn_bq': _L0_attn_in['bq'], 'L0_attn_Wk': _L0_attn_in['Wk'], 'L0_attn_bk': _L0_attn_in['bk'], 'L0_attn_Wv': _L0_attn_in['Wv'], 'L0_attn_bv': _L0_attn_in['bv'], 'L0_attn_Wu': _L0_attn_in['Wu'], 'L0_attn_bu': _L0_attn_in['bu'], 'L0_attn_Wo': _L0_attn_in['Wo'], 'L0_attn_bo': _L0_attn_in['bo'], 'L0_attn_scale': _L0_attn_in['scale'], 'L0_ffn_Wg': _L0_ffn_in['Wg'], 'L0_ffn_ln_scale': _L0_ffn_in['ln_scale'], 'L0_ffn_ln_bias': _L0_ffn_in['ln_bias'], 'L0_ffn_W1': _L0_ffn_in['W1'], 'L0_ffn_b1': _L0_ffn_in['b1'], 'L0_ffn_W2': _L0_ffn_in['W2'], 'L0_ffn_b2': _L0_ffn_in['b2']}
    _x0 = _d['L0_attn_x']
    _d['L0_attn_x'] = jax.random.normal(jax.random.fold_in(jax.random.key(seed), 1), (2, 2048, 256), dtype=_x0.dtype)
    del _x0
    return _d

def reference(L0_attn_x, L0_attn_Wq, L0_attn_bq, L0_attn_Wk, L0_attn_bk, L0_attn_Wv, L0_attn_bv, L0_attn_Wu, L0_attn_bu, L0_attn_Wo, L0_attn_bo, L0_attn_scale, L0_ffn_Wg, L0_ffn_ln_scale, L0_ffn_ln_bias, L0_ffn_W1, L0_ffn_b1, L0_ffn_W2, L0_ffn_b2):

    def _L0_attn_ref(x, Wq, bq, Wk, bk, Wv, bv, Wu, bu, Wo, bo, scale):
        import jax, jax.numpy as jnp
        import numpy as np
        B, N, E, H = (2, 512, 256, 8)
        HID = 256
        D = HID // H
        EPS = 1e-08

        def rms_norm(x, scale):
            rms = jnp.linalg.norm(x, axis=-1, keepdims=True) * x.shape[-1] ** (-0.5)
            return scale * (x / (rms + EPS))
        n = x.shape[-2]
        q = x @ Wq.T + bq
        u = x @ Wu.T + bu
        k = x @ Wk.T + bk
        v = x @ Wv.T + bv
        u = jax.nn.silu(u)
        v = jax.nn.silu(v)
        to_heads = lambda t: t.reshape(*t.shape[:-1], H, D).swapaxes(-3, -2)
        q, k, v = map(to_heads, (q, k, v))
        q = jax.nn.elu(q)
        k = jax.nn.elu(k)
        mask = jnp.tril(jnp.ones((n, n), q.dtype))
        energy = jnp.einsum('bhnd,bhmd->bhnm', q, k) * mask
        out = jnp.einsum('bhnm,bhmd->bhnd', energy, v)
        out = out.swapaxes(-3, -2).reshape(*x.shape[:-1], HID)
        out = rms_norm(out, scale)
        out = u * out
        return out @ Wo.T + bo

    def _L0_ffn_ref(x, Wg, ln_scale, ln_bias, W1, b1, W2, b2):
        import jax, jax.numpy as jnp
        import numpy as np
        B, T, D, E, H = (8, 512, 256, 8, 64)
        LN_EPS = 1e-05
        Bs, Ts, Ds = x.shape
        xt = x.reshape(Bs * Ts, Ds)
        logits = xt @ Wg.T
        top1 = jnp.argmax(logits, axis=-1)
        mu = jnp.mean(xt, axis=-1, keepdims=True)
        var = jnp.mean(jnp.square(xt - mu), axis=-1, keepdims=True)
        xhat = (xt - mu) * jax.lax.rsqrt(var + LN_EPS)
        n_experts = Wg.shape[0]

        def body(y, p):
            s_e, b_e, w1, bb1, w2, bb2, eid = p
            h = jax.nn.gelu((xhat * s_e + b_e) @ w1 + bb1, approximate=False)
            out = h @ w2 + bb2
            mask = (top1 == eid)[:, None].astype(out.dtype)
            return (y + mask * out, None)
        y0 = jnp.zeros_like(xt)
        y, _ = jax.lax.scan(body, y0, (ln_scale, ln_bias, W1, b1, W2, b2, jnp.arange(n_experts)))
        return y.reshape(Bs, Ts, Ds)
    x = L0_attn_x
    xn = _layernorm(x, axis=-1)
    x = x + _L0_attn_ref(xn, L0_attn_Wq, L0_attn_bq, L0_attn_Wk, L0_attn_bk, L0_attn_Wv, L0_attn_bv, L0_attn_Wu, L0_attn_bu, L0_attn_Wo, L0_attn_bo, L0_attn_scale) + _L0_ffn_ref(xn, L0_ffn_Wg, L0_ffn_ln_scale, L0_ffn_ln_bias, L0_ffn_W1, L0_ffn_b1, L0_ffn_W2, L0_ffn_b2)
    return x

_drawn_inputs = setup_inputs


def setup_inputs(seed=0):
    import zlib

    import numpy as np

    out = dict(_drawn_inputs(seed))
    spreads = {'L0_attn_bq': (0.0, 0.596),
     'L0_attn_bk': (0.0, 0.1),
     'L0_attn_bv': (0.0, 0.1),
     'L0_attn_bu': (0.0, 0.446),
     'L0_attn_bo': (0.0, 0.1),
     'L0_attn_scale': (1.0, 0.6),
     'L0_ffn_ln_scale': (1.0, 0.6),
     'L0_ffn_ln_bias': (0.0, 2.0),
     'L0_ffn_b1': (0.0, 0.8),
     'L0_ffn_b2': (0.0, 0.1)}
    factors = {}
    for name, (base, spread) in spreads.items():
        noise = np.random.default_rng([zlib.crc32(name.encode()), seed]).standard_normal(out[name].shape)
        drawn = base * np.exp(spread * noise) if base else spread * noise
        out[name] = jnp.asarray(drawn.astype(out[name].dtype))
    for name, factor in factors.items():
        out[name] = (out[name] * factor).astype(out[name].dtype)
    return out
```

```python
import concourse.bass as bass
from concourse import mybir
from contextlib import ExitStack

F32 = mybir.dt.float32
F32R = mybir.dt.float32r
BF16 = mybir.dt.bfloat16
ALU = mybir.AluOpType
ACT = mybir.ActivationFunctionType
AX = mybir.AxisListType

B, T, D = 2, 2048, 256
HEADS, DH = 8, 32
NE, HE = 8, 64
P = 128
CH = 4
NT = CH * P
STEPS = B * T // NT
KT = D // P
HPG = P // DH
MT = NE * HE // P
LN_EPS = 1e-5
RMS_EPS = 1e-8
OFF = -1e30

ENGINES = ("pe", "act", "dve", "pool")


class Counts:

    def __init__(self, me, eng, sems, body=None):
        self.me, self.eng, self.sems, self.body = me, eng, sems, body
        self.count = {n: 0 for n in sems}
        self.start = {n: 0 for n in sems}
        self.marks = {}
        self.i = None
        self.waited = {}
        self.scaled = {}

    def value(self, sem, count):
        if self.i is None:
            return count
        return self.scaled[sem] + (self.start[sem] + count)

    def wait(self, *names, apart=False):
        issued = False
        for name in names:
            if name not in self.marks:
                continue
            sem, count = self.marks[name]
            if self.me and count > self.waited.get(sem, -10 ** 9):
                self.waited[sem] = count
                if self.i is not None or count > 0:
                    self.eng.wait_ge(self.sems[sem], self.value(sem, count))
                    issued = True
                    if self.me == "sp" and self.i is not None:
                        self.eng.sem_inc(self.apart["sp"], 1)
        if apart and issued and self.me != "sp" and self.i is not None:
            self.eng.sem_inc(self.apart[self.me], 1)

    def op(self, who, issue, after=(), mark=None, apart=False):
        ins = None
        if who == self.me:
            self.wait(*after, apart=apart)
            ins = issue(self.eng)
        if mark:
            if ins is not None:
                ins.then_inc(self.sems[who], 1)
            self.count[who] += 1
            self.marks[mark] = (who, self.count[who])

    def dma(self, who, sem, issue, after=(), n=1):
        if who == self.me:
            self.wait(*after, apart=True)
            for ins in issue(self.eng):
                ins.then_inc(self.sems[sem], 16)
        self.count[sem] += 16 * n
        self.marks[sem] = (sem, self.count[sem])

    def loop(self, times, body):
        per = {n: self.body["count"][n] if self.body else 0 for n in self.sems}
        if self.me in ENGINES:
            self.eng.drain().then_inc(self.sems[self.me], per[self.me])
        for n in self.sems:
            if n not in ENGINES and per[n] and self.me == "sp":
                self.eng.sem_inc(self.sems[n], per[n])
            self.count[n] += per[n]
            if n in ENGINES and self.me:
                self.eng.wait_ge(self.sems[n], self.count[n])
        self.start, before = dict(self.count), dict(self.count)
        self.count = {n: 0 for n in self.sems}
        if self.body:
            self.marks = {name: (sem, count - per[sem]) for name, (sem, count) in self.body["marks"].items()}
        if self.me:
            with self.eng.Fori(0, times) as i:
                self.i, self.waited = i, {}
                self.scaled = {n: self.eng.snap(i * per[n]) if per[n] else 0 for n in self.uses}
                body()
        else:
            body()
            self.found = {"count": dict(self.count), "marks": dict(self.marks)}
            per = self.count
        self.i, self.waited = None, {}
        last = {n: before[n] + (times - 1) * per[n] for n in self.sems}
        self.marks = {name: (sem, count + last[sem]) for name, (sem, count) in self.marks.items()}
        self.count = {n: before[n] + times * per[n] for n in self.sems}


def build(nc, ins, out):
    ctx = ExitStack()
    with ctx:
        def sb(name, shape, dt=F32):
            return ctx.enter_context(nc.sbuf_tensor(name, shape, dt))

        def bank(name):
            return ctx.enter_context(nc.psum_tensor(name, [P, 512], F32))

        ident = sb("ident", [P, P])
        causal = sb("causal", [P, HPG, P])
        diag = sb("diag", [P, KT, P])
        ones = sb("ones", [P, P])
        half_pow = sb("half_pow", [P, CH])
        inv_half_pow = sb("inv_half_pow", [P, CH])
        rank = sb("rank", [P, CH, NE])
        expert_off = sb("expert_off", [P, NE, HE], BF16)
        w_hi = sb("w_hi", [P, KT, 4, D], F32R)
        w_lo = sb("w_lo", [P, KT, 4, D], F32R)
        wo_hi = sb("wo_hi", [P, KT, D], F32R)
        wo_lo = sb("wo_lo", [P, KT, D], F32R)
        w1_hi = sb("w1_hi", [P, KT, NE * HE], F32R)
        w1_lo = sb("w1_lo", [P, KT, NE * HE], F32R)
        w2_hi = sb("w2_hi", [P, MT, D], F32R)
        w2_lo = sb("w2_lo", [P, MT, D], F32R)
        wg_hi = sb("wg_hi", [P, KT, P], F32R)
        wg_lo = sb("wg_lo", [P, KT, P], F32R)
        b2_hi = sb("b2_hi", [P, D], F32R)
        b2_lo = sb("b2_lo", [P, D], F32R)
        vec_rows = sb("vec_rows", [16, P])
        vecs = sb("vecs", [P, 16])
        ln_rows = sb("ln_rows", [NE, 2, D])
        ln_cols = sb("ln_cols", [P, 2, KT, NE])
        wg_rows = sb("wg_rows", [NE, D])
        h_bias = sb("h_bias", [P, MT])
        x_in = [sb(f"x_in{b}", [P, CH, D]) for b in (0, 1)]
        xn = sb("xn", [P, CH, D])
        xn_hi = sb("xn_hi", [P, KT, NT], F32R)
        xn_lo = sb("xn_lo", [P, KT, NT], F32R)
        xh_hi = sb("xh_hi", [P, KT, NT], F32R)
        xh_lo = sb("xh_lo", [P, KT, NT], F32R)
        pre = [sb(f"pre{j}", [P, NT]) for j in (0, 1)]
        act_out = [sb(f"act_out{j}", [P, NT]) for j in (0, 1)]
        kT = [sb(f"kT{b}", [P, KT, NT]) for b in (0, 1)]
        qT = [sb(f"qT{b}", [P, KT, NT]) for b in (0, 1)]
        uT = [sb(f"uT{b}", [P, KT, NT]) for b in (0, 1)]
        vT = sb("vT", [P, KT, NT])
        q_heads = sb("q_heads", [P, KT, HPG, NT])
        k_tok = sb("k_tok", [P, CH, D])
        v_tok = sb("v_tok", [P, CH, D])
        energy = [sb(f"energy{c}", [P, KT, 512]) for c in (0, 1)]
        state = [sb(f"state{b}", [P, D]) for b in (0, 1)]
        kv_new = sb("kv_new", [P, D])
        g = sb("g", [P, KT, NT])
        g_hi = sb("g_hi", [P, KT, NT], F32R)
        g_lo = sb("g_lo", [P, KT, NT], F32R)
        h = [sb(f"h{j}", [P, NT]) for j in (0, 1)]
        h_hi = sb("h_hi", [P, MT, NT], F32R)
        h_lo = sb("h_lo", [P, MT, NT], F32R)
        ya = sb("ya", [P, KT, NT])
        yf = sb("yf", [P, KT, NT])
        sq = ya
        x_res = sb("x_res", [P, CH, D])
        o = sb("o", [P, CH, D])
        off_T = [sb(f"off_T{b}", [P, NT], BF16) for b in (0, 1)]
        on_T = [sb(f"on_T{b}", [P, NT], F32R) for b in (0, 1)]
        logit_T = sb("logit_T", [P, NT])
        onehot = sb("onehot", [P, CH, NE])
        hit = sb("hit", [P, CH, NE])
        top = sb("top", [P, CH])
        win = sb("win", [P, CH])
        ssq = sb("ssq", [P, NT])
        stats = [sb(f"stats{j}", [P, CH, 6]) for j in (0, 1)]
        mv = [sb(f"mv{j}", [P, CH, 2]) for j in (0, 1)]
        eps_var = [sb(f"eps_var{j}", [P, CH]) for j in (0, 1)]
        neg_mean = [sb(f"neg_mean{j}", [P, CH]) for j in (0, 1)]
        rstd = [sb(f"rstd{j}", [P, CH]) for j in (0, 1)]
        shift = [sb(f"shift{j}", [P, CH]) for j in (0, 1)]
        ms = sb("ms", [P, CH])
        rms = sb("rms", [P, CH])
        rinv = sb("rinv", [P, CH])
        w_raw = {"k": energy[0][:, 0, :], "v": energy[0][:, 1, :], "q": energy[1][:, 0, :], "u": energy[1][:, 1, :],
                 "o": o[:, 0:2, :].rearrange("p c d -> p (c d)")}
        w1_raw, w2_raw, b2_raw = x_res[:, :, :].rearrange("p c d -> p (c d)"), g[:, :, :], kv_new
        w1_sc, wo_sc = yf[:, :, :], h[0]

        ring = [bank(f"ring{r}") for r in range(3)]
        e_bank = [bank(f"energy_bank{t}") for t in range(KT)]
        o_bank = [bank(f"att_bank{t}") for t in range(KT)]
        kv_bank = bank("kv_bank")

        dma_sems = ["w_k", "w_v", "w_q", "w_u", "w_o", "w_1", "w_2", "w_small", "x_even", "x_odd", "heads",
                    "res", "store"]
        sems = {n: ctx.enter_context(nc.semaphore(f"s_{n}")) for n in list(ENGINES) + dma_sems}

        apart = {n: ctx.enter_context(nc.semaphore(f"s_apart_{n}")) for n in ("dve", "pool", "sp")}

        x_steps = ins["x"].rearrange("b (i c p) d -> i b p c d", c=CH, p=P)
        out_steps = out.rearrange("b (i c p) d -> i b p c d", c=CH, p=P)

        def f32(ap):
            return ap.bitcast(F32)

        def schedule(c):
            op, dma = c.op, c.dma
            turn = [0]

            def next_bank():
                r = turn[0] % len(ring)
                turn[0] += 1
                return ring[r], f"ring{r} free"

            def split(dst_hi, dst_lo, src, after, free, name, src_is_scaled=False):
                op("act", lambda e: e.activation(dst_hi, src, ACT.Copy), after=after, mark=f"{name} hi")
                op("dve", lambda e: e.tensor_tensor(dst_lo, src, f32(dst_hi), ALU.subtract),
                   after=(f"{name} hi",), mark=f"{name} split")
                if free:
                    c.marks[free] = c.marks[f"{name} split"]

            def load_x(i, b):
                dma("sp", ("x_even", "x_odd")[b], lambda e: [e.dma_start(x_in[b][:, :, :], x_steps[i, b])],
                    after=(f"xh{b} transposed",))

            def norm(b, j, src, dst, src_ready, dst_free):
                def stat(e):
                    for k in range(CH):
                        last = e.bn_stats(stats[j][:, k, :], src[:, k, :])
                    return last
                op("dve", stat, after=src_ready, mark=f"stats{j}")

                def aggr(e):
                    for k in range(CH):
                        last = e.bn_aggr(mv[j][:, k, :], stats[j][:, k, :])
                    return last
                op("dve", aggr, after=(f"stats{j}", f"norm{j} scalars"), mark=f"mv{j}", apart=True)
                op("pool", lambda e: e.tensor_scalar(eps_var[j][:, :], mv[j][:, :, 1], LN_EPS, 1.0, ALU.add, ALU.mult),
                   after=(f"mv{j}",), mark=f"eps_var{j}", apart=True)
                op("pool", lambda e: e.tensor_scalar(neg_mean[j][:, :], mv[j][:, :, 0], -1.0, 1.0, ALU.mult, ALU.mult),
                   mark=f"neg_mean{j}")
                op("pool", lambda e: e.tensor_tensor(rstd[j][:, :], eps_var[j][:, :], inv_half_pow[:, :], ALU.pow),
                   after=(f"eps_var{j}",), mark=f"rstd{j}")
                op("pool", lambda e: e.tensor_tensor(shift[j][:, :], neg_mean[j][:, :], rstd[j][:, :], ALU.mult),
                   after=(f"rstd{j}", f"neg_mean{j}"), mark=f"norm{j} scalars")

                def apply(e):
                    for k in range(CH):
                        last = e.tensor_scalar(dst[:, k, :], src[:, k, :], rstd[j][:, k:k + 1], shift[j][:, k:k + 1],
                                               ALU.mult, ALU.add)
                    return last
                op("pool", apply, after=(f"norm{j} scalars",) + dst_free, mark=f"norm{j} done", apart=True)

            def norm_x(b):
                norm(b, 0, x_in[b], xn, (("x_even", "x_odd")[b],), ("xn transposed",))

            def norm_again(b):
                norm(b, 1, xn, x_in[b], ("norm0 done",), ())
                c.marks[f"xh{b} ready"] = c.marks["norm1 done"]

            def transpose_tokens(src, t, name, ready, done=None):
                bk, free = next_bank()

                def go(e):
                    for k in range(CH):
                        last = e.transpose(bk[:, k * P:(k + 1) * P], src[:, k, t * P:(t + 1) * P], ident[:, :])
                    return last
                op("pe", go, after=(ready, free), mark=name)
                return bk, free

            def transpose_xn(t):
                bk, free = transpose_tokens(xn, t, f"xn T{t}", "norm0 done")
                c.marks["xn transposed"] = c.marks[f"xn T{t}"]
                split(xn_hi[:, t, :], xn_lo[:, t, :], bk[:, :], (f"xn T{t}", "projected"), free, f"xnT{t}")

            def transpose_xh(b, t):
                bk, free = transpose_tokens(x_in[b], t, f"xh T{t}", f"xh{b} ready")
                c.marks[f"xh{b} transposed"] = c.marks[f"xh T{t}"]
                split(xh_hi[:, t, :], xh_lo[:, t, :], bk[:, :], (f"xh T{t}", "hidden products"), free, f"xhT{t}")

            def products(bk, passes, first=True, last=True):
                def go(e):
                    for n, (w, x) in enumerate(passes):
                        ins_ = e.matmul(bk, w, x, start=(n == 0), stop=(n == len(passes) - 1))
                    return ins_
                return go

            def three(w_h, w_l, x_h, x_l, tiles):
                out_ = []
                for k in range(tiles):
                    out_ += [(w_h(k), x_h(k)), (w_h(k), x_l(k)), (w_l(k), x_h(k))]
                return out_

            def project(b, what, t):
                wi = "kvqu".index(what)
                j = t
                bk, free = next_bank()
                name = f"{what}{t}"
                rows = slice(t * P, (t + 1) * P)
                op("pe", products(bk[:, :], three(lambda k: w_hi[:, k, wi, rows], lambda k: w_lo[:, k, wi, rows],
                                                  lambda k: xn_hi[:, k, :], lambda k: xn_lo[:, k, :], KT)),
                   after=("xnT0 split", "xnT1 split", free), mark=f"{name} product")
                c.marks["projected"] = c.marks[f"{name} product"]
                op("act", lambda e: e.activation(pre[j][:, :], bk[:, :], ACT.Identity,
                                                 bias=vecs[:, 2 * wi + t:2 * wi + t + 1]),
                   after=(f"{name} product", f"pre{j} used"), mark=f"{name} pre")
                c.marks[free] = c.marks[f"{name} pre"]
                dst = {"k": kT[b], "v": vT, "q": qT[b], "u": uT[b]}[what]
                if what in "kq":
                    op("act", lambda e: e.activation(act_out[j][:, :], pre[j][:, :], ACT.Exp),
                       after=(f"{name} pre",), mark=f"{name} exp")
                    op("dve", lambda e: e.tensor_scalar(pre[j][:, :], pre[j][:, :], -1.0, -1.0, ALU.add, ALU.max),
                       after=(f"{name} exp",), mark=f"{name} linear")
                    op("dve", lambda e: e.scalar_tensor_tensor(dst[:, t, :], act_out[j][:, :], 1.0, pre[j][:, :],
                                                               ALU.min, ALU.add),
                       after=(f"{name} linear",) + ((f"heads",) if what == "q" else ()), mark=f"{name} ready")
                else:
                    op("act", lambda e: e.activation(act_out[j][:, :], pre[j][:, :], ACT.Tanh, scale=0.5),
                       after=(f"{name} pre",), mark=f"{name} tanh")
                    op("dve", lambda e: e.scalar_tensor_tensor(dst[:, t, :], act_out[j][:, :], 1.0, pre[j][:, :],
                                                               ALU.add, ALU.mult),
                       after=(f"{name} tanh",) + (("v in tokens",) if what == "v" else ()), mark=f"{name} ready")
                c.marks[f"pre{j} used"] = c.marks[f"{name} ready"]

            def spread_heads(b):
                def go(e):
                    return [e.dma_start(q_heads[DH * n:DH * (n + 1), :, n, :], qT[b][DH * n:DH * (n + 1), :, :])
                            for n in range(HPG)]
                dma("sp", "heads", go, after=("q0 ready", "q1 ready", "scores"), n=HPG)

            def gate_logits():
                bk, free = next_bank()
                op("pe", products(bk[:, :], three(lambda k: wg_hi[:, k, :], lambda k: wg_lo[:, k, :],
                                                     lambda k: xn_hi[:, k, :], lambda k: xn_lo[:, k, :], KT)),
                   after=("xnT0 split", "xnT1 split", free), mark="logits")
                c.marks["projected"] = c.marks["logits"]
                op("act", lambda e: e.activation(logit_T[:, :], bk[:, :], ACT.Copy),
                   after=("logits", "logits in tokens"), mark="logit_T")
                c.marks[free] = c.marks["logit_T"]

            def choose_expert():
                bk, free = next_bank()
                lt = bk[:, :].rearrange("p (c n) -> p c n", c=CH)[:, :, 0:NE]

                def go(e):
                    for k in range(CH):
                        last = e.transpose(bk[:, k * P:(k + 1) * P], logit_T[:, k * P:(k + 1) * P], ident[:, :])
                    return last
                op("pe", go, after=("logit_T", free), mark="logits in tokens")
                wide = [P, CH, NE]
                op("dve", lambda e: e.tensor_reduce(top[:, :], lt, AX.X, ALU.max), after=("logits in tokens",),
                   mark="top")
                op("dve", lambda e: e.tensor_tensor(hit[:, :, :], lt, top[:, :].unsqueeze(2).to_broadcast(wide),
                                                    ALU.is_equal), after=("top",), mark="hit")
                c.marks[free] = c.marks["hit"]
                op("dve", lambda e: e.tensor_tensor(hit[:, :, :], hit[:, :, :], rank[:, :, :], ALU.mult),
                   after=("hit",), mark="ranked")
                op("dve", lambda e: e.tensor_reduce(win[:, :], hit[:, :, :], AX.X, ALU.max), after=("ranked",),
                   mark="win")
                op("dve", lambda e: e.tensor_tensor(onehot[:, :, :], hit[:, :, :],
                                                    win[:, :].unsqueeze(2).to_broadcast(wide), ALU.is_equal),
                   after=("win", "onehot transposed"), mark="onehot")

            def gate_rows(b):
                bk, free = next_bank()

                def go(e):
                    for k in range(CH):
                        last = e.transpose(bk[0:NE, k * P:(k + 1) * P], onehot[:, k, :], ident[:, :])
                    return last
                op("pe", go, after=("onehot", free), mark="onehot transposed")
                op("dve", lambda e: e.tensor_scalar(off_T[b][0:NE, :], bk[0:NE, :], -1.0, 1.0, ALU.mult, ALU.add),
                   after=("onehot transposed", "hidden products"), mark="off_T")
                op("dve", lambda e: e.tensor_copy(on_T[b][0:NE, :], bk[0:NE, :]),
                   after=(f"expert products{b}",), mark="on_T")
                c.marks[free] = c.marks["on_T"]

            def to_tokens(src, dst, what, half, ready, dst_free):
                bk, free = next_bank()

                def go(e):
                    for k in (0, 1):
                        for t in range(KT):
                            col = k * D + t * P
                            tok = (2 * half + k) * P
                            last = e.transpose(bk[:, col:col + P], src[:, t, tok:tok + P], ident[:, :])
                    return last
                name = f"{what} T{half}"
                op("pe", go, after=ready + (free,), mark=name)
                c.marks[f"{what} in tokens"] = c.marks[name]
                op("act", lambda e: e.activation(dst[:, 2 * half:2 * half + 2, :].rearrange("p c d -> p (c d)"),
                                                 bk[:, :], ACT.Copy), after=(name,) + dst_free,
                   mark=f"{what}_tok{half}")
                c.marks[free] = c.marks[f"{what}_tok{half}"]

            def scores(b, k):
                for t in range(KT):
                    op("pe", lambda e, t=t: e.matmul(
                        e_bank[t][:, :].rearrange("p (h n) -> p h n", h=HPG),
                        kT[b][:, t, k * P:(k + 1) * P], q_heads[:, t, :, k * P:(k + 1) * P], start=True, stop=True),
                       after=("heads", "k0 ready", "k1 ready", f"energy{t} masked"), mark=f"scores{t}")
                    op("dve", lambda e, t=t: e.tensor_tensor(
                        energy[k % 2][:, t, :], e_bank[t][:, :], causal[:, :, :].rearrange("p h n -> p (h n)"),
                        ALU.mult), after=(f"scores{t}", f"attended{k % 2}"), mark=f"energy{t} masked")
                c.marks["scores"] = c.marks["scores1"]

            def attend(b, k):
                for t in range(KT):
                    def go(e, t=t):
                        tok = slice(k * P, (k + 1) * P)
                        e.matmul(o_bank[t][:, tok], state[b][:, t * P:(t + 1) * P], qT[b][:, t, tok],
                                 start=True, stop=False, skip_group_check=True)
                        for n in range(HPG):
                            last = e.matmul(o_bank[t][DH * n:DH * (n + 1), tok],
                                            v_tok[:, k, t * P + DH * n:t * P + DH * (n + 1)],
                                            energy[k % 2][:, t, P * n:P * (n + 1)],
                                            start=False, stop=True, skip_group_check=True,
                                            tile_position=(0, DH * n))
                        return last
                    op("pe", go, after=(f"energy{t} masked", f"state{b}", "v_tok0", "v_tok1", f"att{t} read"),
                       mark=f"att{t}")
                c.marks[f"attended{k % 2}"] = c.marks["att1"]

                def kv(e):
                    for t in range(KT):
                        cols = slice(t * P, (t + 1) * P)
                        last = e.matmul(kv_bank[:, cols], k_tok[:, k, cols], v_tok[:, k, cols],
                                        start=True, stop=True)
                    return last
                op("pe", kv, after=("k_tok0", "k_tok1", "kv masked"), mark="kv")
                op("dve", lambda e: e.tensor_tensor(kv_new[:, :], kv_bank[:, 0:D],
                                                    diag[:, :, :].rearrange("p t n -> p (t n)"), ALU.mult),
                   after=("kv", f"state{b}"), mark="kv masked")
                op("dve", lambda e: e.tensor_tensor(state[b][:, :], state[b][:, :], kv_new[:, :], ALU.add),
                   after=("kv masked", "att1"), mark=f"state{b}")

            def attention_out(b):
                for t in range(KT):
                    op("act", lambda e, t=t: e.activation(sq[:, t, :], o_bank[t][:, :], ACT.Square),
                       after=(f"att{t}", "ya in tokens"), mark=f"sq{t}")
                    op("dve", lambda e, t=t: e.tensor_tensor(g[:, t, :], o_bank[t][:, :], uT[b][:, t, :], ALU.mult),
                       after=(f"sq{t}", f"u{t} ready", f"g{t} split"), mark=f"g{t}")
                    c.marks[f"att{t} read"] = c.marks[f"g{t}"]
                    op("dve", lambda e, t=t: e.tensor_copy(g_hi[:, t, :], g[:, t, :]),
                       after=(f"g{t}", "wo products"), mark=f"g{t} hi")
                    op("pool", lambda e, t=t: e.tensor_tensor(g_lo[:, t, :], g[:, t, :], f32(g_hi[:, t, :]),
                                                              ALU.subtract),
                       after=(f"g{t} hi",), mark=f"g{t} split")

            def sum_squares():
                bk, free = next_bank()
                op("pe", products(bk[:, :], [(ones[:, :], sq[:, t, :]) for t in range(KT)]),
                   after=("sq0", "sq1", free), mark="ssq product")
                op("act", lambda e: e.activation(ssq[:, :], bk[:, :], ACT.Copy),
                   after=("ssq product", "ssq in tokens"), mark="ssq")
                c.marks[free] = c.marks["ssq"]

            def inverse_rms():
                bk, free = next_bank()

                def go(e):
                    for k in range(CH):
                        last = e.transpose(bk[:, k * P:(k + 1) * P], ssq[:, k * P:(k + 1) * P], ident[:, :])
                    return last
                op("pe", go, after=("ssq", free), mark="ssq in tokens")
                op("dve", lambda e: e.tensor_scalar(ms[:, :], bk[:, :].rearrange("p (c n) -> p c n", c=CH)[:, :, 0], 1.0 / D, None, ALU.mult),
                   after=("ssq in tokens",), mark="ms")
                c.marks[free] = c.marks["ms"]
                op("pool", lambda e: e.tensor_tensor(rms[:, :], ms[:, :], half_pow[:, :], ALU.pow),
                   after=("ms",), mark="rms")
                op("pool", lambda e: e.tensor_scalar(rms[:, :], rms[:, :], RMS_EPS, 1.0, ALU.add, ALU.mult),
                   after=("rms",), mark="rms eps", apart=True)
                op("dve", lambda e: e.reciprocal(rinv[:, :], rms[:, :]), after=("rms eps",), mark="rinv")

            def attention_product(t):
                bk, free = next_bank()
                cols = slice(t * P, (t + 1) * P)
                op("pe", products(bk[:, :], three(lambda k: wo_hi[:, k, cols], lambda k: wo_lo[:, k, cols],
                                                  lambda k: g_hi[:, k, :], lambda k: g_lo[:, k, :], KT)),
                   after=("g0 split", "g1 split", free), mark="wo products")
                op("act", lambda e: e.activation(ya[:, t, :], bk[:, :], ACT.Copy),
                   after=("wo products", "ssq product", "ya in tokens"), mark=f"ya{t}")
                c.marks[free] = c.marks[f"ya{t}"]

            def hidden(b, m):
                bk, free = next_bank()
                cols = slice(m * P, (m + 1) * P)
                j = m % 2
                op("pe", products(bk[:, :], three(lambda k: w1_hi[:, k, cols], lambda k: w1_lo[:, k, cols],
                                                  lambda k: xh_hi[:, k, :], lambda k: xh_lo[:, k, :], KT)
                                  + [(expert_off[:, 2 * m:2 * m + 2, :].rearrange("p e j -> p (e j)"),
                                      off_T[b][:, :])]),
                   after=("xhT0 split", "xhT1 split", "off_T", free), mark="hidden products")
                op("act", lambda e: e.activation(h[j][:, :], bk[:, :], ACT.Gelu, bias=h_bias[:, m:m + 1]),
                   after=("hidden products", f"h{j} split"), mark=f"h{j}")
                c.marks[free] = c.marks[f"h{j}"]
                op("dve", lambda e: e.tensor_copy(h_hi[:, m, :], h[j][:, :]),
                   after=(f"h{j}", "expert products"), mark=f"h{j} hi")
                op("pool", lambda e: e.tensor_tensor(h_lo[:, m, :], h[j][:, :], f32(h_hi[:, m, :]), ALU.subtract),
                   after=(f"h{j} hi",), mark=f"h{j} split")

            def expert_product(b, t):
                bk, free = next_bank()
                cols = slice(t * P, (t + 1) * P)
                op("pe", products(bk[:, :], [(b2_hi[:, cols], on_T[b][:, :]), (b2_lo[:, cols], on_T[b][:, :])]
                                  + three(lambda k: w2_hi[:, k, cols], lambda k: w2_lo[:, k, cols],
                                          lambda k: h_hi[:, k, :], lambda k: h_lo[:, k, :], MT)),
                   after=("on_T", "h0 split", "h1 split", free), mark="expert products")
                c.marks[f"expert products{b}"] = c.marks["expert products"]
                op("act", lambda e: e.activation(yf[:, t, :], bk[:, :], ACT.Identity, bias=vecs[:, 8 + t:9 + t]),
                   after=("expert products", "yf in tokens"), mark=f"yf{t}")
                c.marks[free] = c.marks[f"yf{t}"]

            def load_residual(i, b):
                dma("sp", "res", lambda e: [e.dma_start(x_res[:, :, :], x_steps[i, b])], after=("attention added",))

            def finish(i, b):
                for half in (0, 1):
                    bk, free = next_bank()

                    def tr(src):
                        def go(e):
                            for k in (0, 1):
                                for t in range(KT):
                                    tok = (2 * half + k) * P
                                    last = e.transpose(bk_[:, k * D + t * P:k * D + (t + 1) * P],
                                                       src[:, t, tok:tok + P], ident[:, :])
                            return last
                        return go
                    bk_ = bk
                    op("pe", tr(ya), after=("ya0", "ya1", free), mark="ya in tokens")

                    def add(e):
                        for k in (0, 1):
                            n = 2 * half + k
                            last = e.scalar_tensor_tensor(o[:, n, :], bk[:, k * D:(k + 1) * D], rinv[:, n:n + 1],
                                                          x_res[:, n, :], ALU.mult, ALU.add)
                        return last
                    op("dve", add, after=("ya in tokens", "rinv", "res", "store"), mark="attention added")
                    c.marks[free] = c.marks["attention added"]
                for half in (0, 1):
                    bk, free = next_bank()
                    bk_ = bk
                    op("pe", tr_at(yf, bk, half), after=("yf0", "yf1", free), mark="yf in tokens")
                    both = slice(2 * half, 2 * half + 2)
                    op("dve", lambda e: e.tensor_tensor(o[:, both, :].rearrange("p c d -> p (c d)"),
                                                        o[:, both, :].rearrange("p c d -> p (c d)"), bk[:, :],
                                                        ALU.add),
                       after=("yf in tokens", "attention added"), mark="o")
                    c.marks[free] = c.marks["o"]
                dma("sp", "store", lambda e: [e.dma_start(out_steps[i, b], o[:, :, :])], after=("o",))

            def tr_at(src, bk, half):
                def go(e):
                    for k in (0, 1):
                        for t in range(KT):
                            tok = (2 * half + k) * P
                            last = e.transpose(bk[:, k * D + t * P:k * D + (t + 1) * P],
                                               src[:, t, tok:tok + P], ident[:, :])
                    return last
                return go

            def constants():
                op("pool", lambda e: e.memset(ident[:, :], 0.0), mark="ident 0")
                op("pool", lambda e: e.affine_select(out=ident[:, :], in_=ident[:, :], compare_op=ALU.not_equal,
                                                     fill=1.0, base=0, pattern=[[-1, P]], channel_multiplier=1),
                   after=("ident 0",), mark="ident")
                op("pool", lambda e: e.memset(causal[:, :, :], 0.5), mark="causal 0")
                op("pool", lambda e: e.affine_select(out=causal[:, :, :], in_=causal[:, :, :], compare_op=ALU.is_ge,
                                                     fill=0.0, base=0, pattern=[[0, HPG], [1, P]],
                                                     channel_multiplier=-1),
                   after=("causal 0",), mark="causal")
                op("pool", lambda e: e.memset(expert_off[:, :, :], OFF), mark="expert_off 0")
                op("pool", lambda e: e.affine_select(out=expert_off[:, :, :], in_=expert_off[:, :, :],
                                                     compare_op=ALU.is_equal, fill=0.0, base=0,
                                                     pattern=[[-1, NE], [0, HE]], channel_multiplier=1),
                   after=("expert_off 0",), mark="expert_off")
                op("pool", lambda e: e.memset(half_pow[:, :], 0.5))
                op("pool", lambda e: e.memset(inv_half_pow[:, :], -0.5), mark="powers")

                def zeros(e):
                    e.memset(diag[:, :, :], 0.0)
                    e.memset(ones[:, :], 1.0)
                    for n in range(NE):
                        e.memset(rank[:, :, n:n + 1], float(NE - n))
                    for b in (0, 1):
                        e.memset(state[b][:, :], 0.0)
                        e.memset(off_T[b][:, :], 0.0)
                        e.memset(f32(on_T[b][:, :]), 0.0)
                    e.memset(f32(wg_hi[:, :, :]), 0.0)
                    e.memset(f32(wg_lo[:, :, :]), 0.0)
                    e.memset(f32(b2_hi[:, :]), 0.0)
                    e.memset(f32(b2_lo[:, :]), 0.0)
                    return e.memset(q_heads[:, :, :, :], 0.0)
                op("dve", zeros, mark="zeros")
                for b in (0, 1):
                    c.marks[f"state{b}"] = c.marks["zeros"]

                def blocks(e):
                    for n in range(HPG):
                        last = e.memset(diag[DH * n:DH * (n + 1), :, DH * n:DH * (n + 1)], 0.5)
                    return last
                op("dve", blocks, after=("zeros",), mark="diag")

            def load_weights():
                for what in "kvqu":
                    dma("sp", f"w_{what}", lambda e, what=what: [e.dma_start(
                        w_raw[what].rearrange("p (a e) -> p a e", a=KT),
                        ins[f"W{what}"].rearrange("(a p) e -> p a e", p=P))])
                small = []

                def go(e):
                    for r, n in enumerate(("bk", "bv", "bq", "bu", "bo", "scale")):
                        small.append(e.dma_start(vec_rows[2 * r:2 * r + 2, :], ins[n].rearrange("(r p) -> r p", p=P)))
                    small.append(e.dma_start(vec_rows[12:16, :], ins["b1"].rearrange("(r m) j -> r (m j)", m=2)))
                    small.append(e.dma_start(ln_rows[:, 0, :], ins["ln_scale"]))
                    small.append(e.dma_start(ln_rows[:, 1, :], ins["ln_bias"]))
                    small.append(e.dma_start(wg_rows[:, :], ins["Wg"]))
                    small.append(e.dma_start(b2_raw[0:NE, :], ins["b2"]))
                    return small
                dma("act", "w_small", go, n=11)
                dma("sp", "w_1", lambda e: [e.dma_start(
                    w1_raw.rearrange("p (a x j) -> p a x j", a=KT, x=NE)[:, a, :, :],
                    ins["W1"].rearrange("x (a p) j -> a p x j", p=P)[a]) for a in range(KT)], n=KT)
                dma("sp", "w_o", lambda e: [e.dma_start(w_raw["o"].rearrange("p (a e) -> p a e", a=KT),
                                                        ins["Wo"].rearrange("(a p) e -> p a e", p=P))])
                dma("sp", "w_2", lambda e: [e.dma_start(
                    w2_raw.rearrange("p a (m d) -> p (a m) d", m=2),
                    ins["W2"].rearrange("(m x) j d -> (x j) m d", x=2) if False else
                    ins["W2"].rearrange("x j d -> (x j) d").rearrange("(m p) d -> p m d", p=P))])

            def turn_small():
                bk, free = next_bank()
                ln = bk[:, 16:16 + 2 * KT * NE].rearrange("p (w k e) -> p w k e", w=2, k=KT)
                wg = bk[:, 64:64 + KT * NE].rearrange("p (k e) -> p k e", k=KT)

                def go(e):
                    last = e.transpose(bk[:, 0:16], vec_rows[:, :], ident[0:16, 0:16])
                    for k in range(KT):
                        cols = slice(k * P, (k + 1) * P)
                        for w in (0, 1):
                            last = e.transpose(ln[:, w, k, :], ln_rows[:, w, cols], ident[0:NE, 0:NE])
                        last = e.transpose(wg[:, k, :], wg_rows[:, cols], ident[0:NE, 0:NE])
                    return last
                op("pe", go, after=("ident", "w_small"), mark="small turned")
                op("dve", lambda e: e.tensor_copy(vecs[:, :], bk[:, 0:16]), after=("small turned",))
                op("dve", lambda e: e.tensor_copy(ln_cols[:, :, :, :], ln), mark="small")
                op("dve", lambda e: e.tensor_copy(wg_hi[:, :, 0:NE], wg), after=("zeros",), mark="wg hi")
                op("dve", lambda e: e.tensor_tensor(wg_lo[:, :, 0:NE], wg, f32(wg_hi[:, :, 0:NE]), ALU.subtract),
                   after=("wg hi",), mark="wg")
                c.marks[free] = c.marks["wg"]
                op("dve", lambda e: e.tensor_copy(b2_hi[0:NE, :], b2_raw[0:NE, :]), after=("zeros", "w_small"),
                   mark="b2 hi")
                op("dve", lambda e: e.tensor_tensor(b2_lo[0:NE, :], b2_raw[0:NE, :], f32(b2_hi[0:NE, :]),
                                                    ALU.subtract), after=("b2 hi",), mark="b2")

            def turn_weight(what, k):
                bk, free = next_bank()
                raw = w_raw[what].rearrange("p (a e) -> p a e", a=KT)

                def go(e):
                    for a in range(KT):
                        last = e.transpose(bk[:, a * P:(a + 1) * P], raw[:, a, k * P:(k + 1) * P], ident[:, :])
                    return last
                name = f"W{what}{k}"
                op("pe", go, after=("ident", f"w_{what}", free), mark=f"{name} turned")
                if what == "o":
                    op("dve", lambda e: e.tensor_scalar(wo_sc[:, 0:D], bk[:, 0:D], vecs[:, 10 + k:11 + k], 0.5,
                                                        ALU.mult, ALU.mult),
                       after=(f"{name} turned", "small", f"Wo{k - 1} split"), mark=f"{name} scaled")
                    c.marks[free] = c.marks[f"{name} scaled"]
                    split(wo_hi[:, k, :], wo_lo[:, k, :], wo_sc[:, 0:D], (f"{name} scaled",), None, name)
                else:
                    wi = "kvqu".index(what)
                    split(w_hi[:, k, wi, :], w_lo[:, k, wi, :], bk[:, 0:D], (f"{name} turned",), free, name)

            def expert_weights():
                raw1 = w1_raw.rearrange("p (k n) -> p k n", k=KT)
                for k in range(KT):
                    op("dve", lambda e, k=k: e.tensor_tensor(
                        w1_sc[:, k, :].rearrange("p (x j) -> p x j", x=NE),
                        raw1[:, k, :].rearrange("p (x j) -> p x j", x=NE),
                        ln_cols[:, 0, k, :].unsqueeze(2).to_broadcast([P, NE, HE]), ALU.mult),
                       after=("small", "w_1"), mark=f"W1{k} scaled")
                    split(w1_hi[:, k, :], w1_lo[:, k, :], w1_sc[:, k, :], (f"W1{k} scaled",), None, f"W1{k}")
                raw2 = w2_raw.rearrange("p a (m d) -> p (a m) d", m=2)
                split(w2_hi[:, :, :], w2_lo[:, :, :], raw2, ("w_2",), None, "W2")
                bk, free = next_bank()

                def go(e):
                    for m in range(MT):
                        for k in range(KT):
                            last = e.matmul(bk[:, 2 * m:2 * m + 2], raw1[:, k, m * P:(m + 1) * P],
                                            ln_cols[:, 1, k, 2 * m:2 * m + 2], start=(k == 0), stop=(k == KT - 1))
                    return last
                op("pe", go, after=("small", "w_1", free), mark="ln_bias product")
                pairs = bk[:, 0:2 * MT].rearrange("p (m x) -> p m x", x=2)
                for x in (0, 1):
                    rows = slice(HE * x, HE * (x + 1))
                    op("dve", lambda e, x=x, rows=rows: e.tensor_tensor(
                        h_bias[rows, :], pairs[rows, :, x], vecs[rows, 12:16], ALU.add),
                       after=("ln_bias product",), mark="h_bias")
                c.marks[free] = c.marks["h_bias"]

            def tick(i, b, project_next=True, norm_next=True):
                n = 1 - b
                turn[0] = 0
                ni = i + b
                units = [(w, t) for w in "kvqu" for t in range(KT)]
                load_residual(i, b)
                if norm_next:
                    load_x(i + 1, b)
                for k in range(CH):
                    scores(b, k)
                    if project_next:
                        for w, t in units[2 * k:2 * k + 2]:
                            project(n, w, t)
                    attend(b, k)
                    if k == 0 and norm_next:
                        norm_x(b)
                    if k == 2 and norm_next:
                        norm_again(b)
                if project_next:
                    gate_logits()
                    spread_heads(n)
                attention_out(b)
                hidden(b, 0)
                hidden(b, 1)
                if norm_next:
                    transpose_xn(0)
                    transpose_xn(1)
                sum_squares()
                hidden(b, 2)
                hidden(b, 3)
                if project_next:
                    choose_expert()
                attention_product(0)
                attention_product(1)
                inverse_rms()
                if project_next:
                    for half in (0, 1):
                        to_tokens(kT[n], k_tok, "k", half, ("k0 ready", "k1 ready"), ("kv",))
                    for half in (0, 1):
                        to_tokens(vT, v_tok, "v", half, ("v0 ready", "v1 ready"), ("kv",))
                    transpose_xh(n, 0)
                    transpose_xh(n, 1)
                expert_product(b, 0)
                expert_product(b, 1)
                if project_next:
                    gate_rows(n)
                finish(i, b)

            c.op("act", lambda e: e.preload_act_table(ACT.Exp))
            constants()
            load_weights()
            for b in (0, 1):
                load_x(0, b)
            norm_x(0)
            norm_again(0)
            turn_small()
            for what in "kvqu":
                for k in range(KT):
                    turn_weight(what, k)
            transpose_xn(0)
            transpose_xn(1)
            for w in "kvqu":
                for t in range(KT):
                    project(0, w, t)
            gate_logits()
            spread_heads(0)
            norm_x(1)
            norm_again(1)
            expert_weights()
            for k in range(KT):
                turn_weight("o", k)
            choose_expert()
            transpose_xn(0)
            transpose_xn(1)
            for half in (0, 1):
                to_tokens(kT[0], k_tok, "k", half, ("k0 ready", "k1 ready"), ())
            for half in (0, 1):
                to_tokens(vT, v_tok, "v", half, ("v0 ready", "v1 ready"), ())
            transpose_xh(0, 0)
            transpose_xh(0, 1)
            gate_rows(0)

            pairs = STEPS // 2

            def body():
                tick(c.i if c.i is not None else 0, 0)
                tick(c.i if c.i is not None else 0, 1)
            c.loop(pairs - 1, body)
            tick(pairs - 1, 0, norm_next=False)
            tick(pairs - 1, 1, project_next=False, norm_next=False)
            if c.me == "sp":
                c.wait("store")

        dry = Counts(None, None, sems)
        schedule(dry)
        body = dry.found
        walks = {}
        for me in list(ENGINES) + ["sp"]:
            walks[me] = body
        uses = list(sems)

        block = ctx.enter_context(nc.Block())

        def run(me, eng):
            c = Counts(me, eng, sems, body)
            c.uses = uses
            c.apart = apart
            schedule(c)

        @block.tensor
        def _(eng):
            run("pe", eng)

        @block.scalar
        def _(eng):
            run("act", eng)

        @block.vector
        def _(eng):
            run("dve", eng)

        @block.gpsimd
        def _(eng):
            run("pool", eng)

        @block.sync
        def _(eng):
            run("sp", eng)


def kernel(**inputs):
    import numpy as np
    import concourse.bacc as bacc
    from concourse.bass_utils import run_bass_kernel_spmd

    nc = bacc.Bacc("TRN2", target_bir_lowering=False, num_devices=1)
    arrays, ins = {}, {}
    for name, value in inputs.items():
        a = np.ascontiguousarray(value)
        short = name.replace("L0_attn_", "").replace("L0_ffn_", "")
        arrays[f"in_{short}"] = a
        ins[short] = nc.dram_tensor(f"in_{short}", a.shape, mybir.dt.from_np(a.dtype), kind="ExternalInput").ap()
    out = nc.dram_tensor("out", (B, T, D), F32, kind="ExternalOutput").ap()
    build(nc, ins, out)
    result = run_bass_kernel_spmd(nc, [arrays], core_ids=[0])
    return result.results[0]["out"]
```

```python
import concourse.bass as bass
from concourse import mybir
from contextlib import ExitStack

F32 = mybir.dt.float32
F32R = mybir.dt.float32r
BF16 = mybir.dt.bfloat16
ALU = mybir.AluOpType
ACT = mybir.ActivationFunctionType
AX = mybir.AxisListType

B, T, D = 2, 2048, 256
HEADS, DH = 8, 32
NE, HE = 8, 64
NE_LO = 32
P = 128
CH = 4
NT = CH * P
STEPS = B * T // NT
KT = D // P
HPG = P // DH
MT = NE * HE // P
LN_EPS = 1e-5
RMS_EPS = 1e-8
OFF = -1e30

ENGINES = ("pe", "act", "dve", "pool")


class Counts:

    def __init__(self, me, eng, sems, body=None):
        self.me, self.eng, self.sems, self.body = me, eng, sems, body
        self.count = {n: 0 for n in sems}
        self.start = {n: 0 for n in sems}
        self.marks = {}
        self.i = None
        self.waited = {}
        self.scaled = {}

    def value(self, sem, count):
        if self.i is None:
            return count
        return self.scaled[sem] + (self.start[sem] + count)

    def wait(self, *names, apart=False):
        issued = False
        for name in names:
            if name not in self.marks:
                continue
            sem, count = self.marks[name]
            if self.me and count > self.waited.get(sem, -10 ** 9):
                self.waited[sem] = count
                if self.i is not None or count > 0:
                    self.eng.wait_ge(self.sems[sem], self.value(sem, count))
                    issued = True
                    if self.me == "sp" and self.i is not None:
                        self.eng.sem_inc(self.apart["sp"], 1)
        if apart and issued and self.me != "sp" and self.i is not None:
            self.eng.sem_inc(self.apart[self.me], 1)

    def op(self, who, issue, after=(), mark=None, apart=False):
        ins = None
        if who == self.me:
            self.wait(*after, apart=apart)
            ins = issue(self.eng)
        if mark:
            if ins is not None:
                ins.then_inc(self.sems[who], 1)
            self.count[who] += 1
            self.marks[mark] = (who, self.count[who])

    def dma(self, who, sem, issue, after=(), n=1):
        if who == self.me:
            self.wait(*after, apart=True)
            for ins in issue(self.eng):
                ins.then_inc(self.sems[sem], 16)
        self.count[sem] += 16 * n
        self.marks[sem] = (sem, self.count[sem])

    def loop(self, times, body):
        per = {n: self.body["count"][n] if self.body else 0 for n in self.sems}
        if self.me in ENGINES:
            self.eng.drain().then_inc(self.sems[self.me], per[self.me])
        for n in self.sems:
            if n not in ENGINES and per[n] and self.me == "sp":
                self.eng.sem_inc(self.sems[n], per[n])
            self.count[n] += per[n]
            if n in ENGINES and self.me:
                self.eng.wait_ge(self.sems[n], self.count[n])
        self.start, before = dict(self.count), dict(self.count)
        self.count = {n: 0 for n in self.sems}
        if self.body:
            self.marks = {name: (sem, count - per[sem]) for name, (sem, count) in self.body["marks"].items()}
        if self.me:
            with self.eng.Fori(0, times) as i:
                self.i, self.waited = i, {}
                self.scaled = {n: self.eng.snap(i * per[n]) if per[n] else 0 for n in self.uses}
                body()
        else:
            body()
            self.found = {"count": dict(self.count), "marks": dict(self.marks)}
            per = self.count
        self.i, self.waited = None, {}
        last = {n: before[n] + (times - 1) * per[n] for n in self.sems}
        self.marks = {name: (sem, count + last[sem]) for name, (sem, count) in self.marks.items()}
        self.count = {n: before[n] + times * per[n] for n in self.sems}


def build(nc, ins, out):
    ctx = ExitStack()
    with ctx:
        def sb(name, shape, dt=F32):
            return ctx.enter_context(nc.sbuf_tensor(name, shape, dt))

        def bank(name):
            return ctx.enter_context(nc.psum_tensor(name, [P, 512], F32))

        ident = sb("ident", [P, P])
        causal = sb("causal", [P, HPG, P])
        diag = sb("diag", [P, KT, P])
        ones = sb("ones", [P, P])
        half_pow = sb("half_pow", [P, CH])
        inv_half_pow = sb("inv_half_pow", [P, CH])
        rank = sb("rank", [P, CH, NE])
        expert_off = sb("expert_off", [P, NE, HE], BF16)
        w_hi = sb("w_hi", [P, KT, 4, D], F32R)
        w_lo = sb("w_lo", [P, KT, 4, D], F32R)
        wo_hi = sb("wo_hi", [P, KT, D], F32R)
        wo_lo = sb("wo_lo", [P, KT, D], F32R)
        w1_hi = sb("w1_hi", [P, KT, NE * HE], F32R)
        w1_lo = sb("w1_lo", [P, KT, NE * HE], F32R)
        w2_hi = sb("w2_hi", [P, MT, D], F32R)
        w2_lo = sb("w2_lo", [P, MT, D], F32R)
        wg = sb("wg", [P, KT, P], F32R)
        b2 = sb("b2", [P, D], F32R)
        cols = sb("cols", [P, 16 + 3 * KT * NE])
        vecs = cols[:, 0:16]
        ln_cols = cols[:, 16:16 + 2 * KT * NE].rearrange("p (w k e) -> p w k e", w=2, k=KT)
        wg_cols = cols[:, 16 + 2 * KT * NE:].rearrange("p (k e) -> p k e", k=KT)
        h_bias = sb("h_bias", [P, MT])
        x_in = [sb(f"x_in{b}", [P, CH, D]) for b in (0, 1)]
        xn = sb("xn", [P, CH, D])
        xn_hi = sb("xn_hi", [P, KT, NT], F32R)
        xn_lo = sb("xn_lo", [P, KT, NT], F32R)
        xh_hi = sb("xh_hi", [P, KT, NT], F32R)
        xh_lo = sb("xh_lo", [P, KT, NT], F32R)
        pre = [sb(f"pre{j}", [P, NT]) for j in (0, 1)]
        act_out = [sb(f"act_out{j}", [P, NT]) for j in (0, 1)]
        kT = [sb(f"kT{b}", [P, KT, NT]) for b in (0, 1)]
        qT = [sb(f"qT{b}", [P, KT, NT]) for b in (0, 1)]
        uT = [sb(f"uT{b}", [P, KT, NT]) for b in (0, 1)]
        vT = sb("vT", [P, KT, NT])
        q_heads = sb("q_heads", [P, KT, HPG, NT])
        k_tok = sb("k_tok", [P, CH, D])
        v_tok = sb("v_tok", [P, CH, D])
        energy = [sb(f"energy{c}", [P, KT, 512]) for c in (0, 1)]
        state = [sb(f"state{b}", [P, D]) for b in (0, 1)]
        kv_new = sb("kv_new", [P, D])
        g = sb("g", [P, KT, NT])
        g_hi = sb("g_hi", [P, KT, NT], F32R)
        g_lo = sb("g_lo", [P, KT, NT], F32R)
        h = [sb(f"h{j}", [P, NT]) for j in (0, 1)]
        h_hi = sb("h_hi", [P, MT, NT], F32R)
        h_lo = sb("h_lo", [P, MT, NT], F32R)
        ya = sb("ya", [P, KT, NT])
        yf = sb("yf", [P, KT, NT])
        sq = ya
        x_res = sb("x_res", [P, CH, D])
        o = sb("o", [P, CH, D])
        off_T = [sb(f"off_T{b}", [P, NT], BF16) for b in (0, 1)]
        on_T = [sb(f"on_T{b}", [P, NT], F32R) for b in (0, 1)]
        logit_T = sb("logit_T", [P, NT])
        onehot = sb("onehot", [P, CH, P])
        logit = sb("logit", [P, CH, NE])
        hit = sb("hit", [P, CH, NE])
        top = sb("top", [P, CH])
        win = sb("win", [P, CH])
        ssq = sb("ssq", [P, NT])
        stats = [sb(f"stats{j}", [P, CH, 6]) for j in (0, 1)]
        mv = [sb(f"mv{j}", [P, CH, 2]) for j in (0, 1)]
        eps_var = [sb(f"eps_var{j}", [P, CH]) for j in (0, 1)]
        neg_mean = [sb(f"neg_mean{j}", [P, CH]) for j in (0, 1)]
        rstd = [sb(f"rstd{j}", [P, CH]) for j in (0, 1)]
        shift = [sb(f"shift{j}", [P, CH]) for j in (0, 1)]
        ms = sb("ms", [P, CH])
        rms = sb("rms", [P, CH])
        rinv = sb("rinv", [P, CH])
        w_raw = {"k": energy[0][:, 0, :], "v": energy[0][:, 1, :], "q": energy[1][:, 0, :], "u": energy[1][:, 1, :]}
        w1_raw, w2_raw = x_res[:, :, :].rearrange("p c d -> p (c d)"), g[:, :, :].rearrange("p k n -> p (k n)")
        wo_raw, b2_raw = o[:, 0:KT, :].rearrange("p c d -> p (c d)"), kv_new
        w1_sc, wo_sc = yf[:, :, :], h[0]

        ring = [bank(f"ring{r}") for r in range(3)]
        e_bank = [bank(f"energy_bank{t}") for t in range(KT)]
        o_bank = [bank(f"att_bank{t}") for t in range(KT)]
        kv_bank = bank("kv_bank")

        dma_sems = ["w_k", "w_v", "w_q", "w_u", "w_o", "w_1", "w_2", "w_small", "x_even", "x_odd", "heads",
                    "res", "store"]
        sems = {n: ctx.enter_context(nc.semaphore(f"s_{n}")) for n in list(ENGINES) + dma_sems}

        apart = {n: ctx.enter_context(nc.semaphore(f"s_apart_{n}")) for n in ("dve", "pool", "sp")}

        x_steps = ins["x"].rearrange("b (i c p) d -> i b p c d", c=CH, p=P)
        out_steps = out.rearrange("b (i c p) d -> i b p c d", c=CH, p=P)

        def f32(ap):
            return ap.bitcast(F32)

        def schedule(c):
            op, dma = c.op, c.dma
            turn = [0]

            def next_bank():
                r = turn[0] % len(ring)
                turn[0] += 1
                return ring[r], f"ring{r} free"

            def split(dst_hi, dst_lo, src, after, free, name, rounds="act", who="dve"):
                if rounds == "act":
                    op("act", lambda e: e.activation(dst_hi, src, ACT.Copy), after=after, mark=f"{name} hi")
                else:
                    op("dve", lambda e: e.tensor_copy(dst_hi, src), after=after, mark=f"{name} hi")
                op(who, lambda e: e.tensor_tensor(dst_lo, src, f32(dst_hi), ALU.subtract),
                   after=(f"{name} hi",), mark=f"{name} split")
                if free:
                    c.marks[free] = c.marks[f"{name} split"]

            def load_x(i, b):
                dma("sp", ("x_even", "x_odd")[b], lambda e: [e.dma_start(x_in[b][:, :, :], x_steps[i, b])],
                    after=(f"xh{b} transposed",))

            def norm(b, j, src, dst, src_ready, dst_free, who, meanwhile=lambda: None):
                def stat(e):
                    for k in range(CH):
                        last = e.bn_stats(stats[j][:, k, :], src[:, k, :])
                    return last
                op("dve", stat, after=src_ready, mark=f"stats{j}")

                def aggr(e):
                    for k in range(CH):
                        last = e.bn_aggr(mv[j][:, k, :], stats[j][:, k, :])
                    return last
                op("dve", aggr, after=(f"stats{j}", f"norm{j} scalars"), mark=f"mv{j}", apart=True)
                op("pool", lambda e: e.tensor_scalar(eps_var[j][:, :], mv[j][:, :, 1], LN_EPS, 1.0, ALU.add, ALU.mult),
                   after=(f"mv{j}",), mark=f"eps_var{j}", apart=True)
                op("pool", lambda e: e.tensor_scalar(neg_mean[j][:, :], mv[j][:, :, 0], -1.0, 1.0, ALU.mult, ALU.mult),
                   mark=f"neg_mean{j}")
                op("pool", lambda e: e.tensor_tensor(rstd[j][:, :], eps_var[j][:, :], inv_half_pow[:, :], ALU.pow),
                   after=(f"eps_var{j}",), mark=f"rstd{j}")
                op("pool", lambda e: e.tensor_tensor(shift[j][:, :], neg_mean[j][:, :], rstd[j][:, :], ALU.mult),
                   after=(f"rstd{j}", f"neg_mean{j}"), mark=f"norm{j} scalars")

                meanwhile()

                def apply(e):
                    for k in range(CH):
                        last = e.tensor_scalar(dst[:, k, :], src[:, k, :], rstd[j][:, k:k + 1], shift[j][:, k:k + 1],
                                               ALU.mult, ALU.add)
                    return last
                op(who, apply, after=(f"norm{j} scalars",) + dst_free, mark=f"norm{j} done", apart=(who == "pool"))

            def norm_x(b, who="pool", **meanwhile):
                norm(b, 0, x_in[b], xn, (("x_even", "x_odd")[b],), ("xn transposed",), who, **meanwhile)

            def norm_again(b, who="pool", **meanwhile):
                norm(b, 1, xn, x_in[b], ("norm0 done",), (), who, **meanwhile)
                c.marks[f"xh{b} ready"] = c.marks["norm1 done"]

            def transpose_tokens(src, t, name, ready, done=None):
                bk, free = next_bank()

                def go(e):
                    for k in range(CH):
                        last = e.transpose(bk[:, k * P:(k + 1) * P], src[:, k, t * P:(t + 1) * P], ident[:, :])
                    return last
                op("pe", go, after=(ready, free), mark=name)
                return bk, free

            def transpose_xn(t):
                bk, free = transpose_tokens(xn, t, f"xn T{t}", "norm0 done")
                c.marks["xn transposed"] = c.marks[f"xn T{t}"]
                split(xn_hi[:, t, :], xn_lo[:, t, :], bk[:, :], (f"xn T{t}", "projected"), free, f"xnT{t}")

            def transpose_xh(b, t):
                bk, free = transpose_tokens(x_in[b], t, f"xh T{t}", f"xh{b} ready")
                c.marks[f"xh{b} transposed"] = c.marks[f"xh T{t}"]
                split(xh_hi[:, t, :], xh_lo[:, t, :], bk[:, :], (f"xh T{t}", "hidden products"), free, f"xhT{t}")

            def products(bk, passes, first=True, last=True):
                def go(e):
                    for n, (w, x) in enumerate(passes):
                        ins_ = e.matmul(bk, w, x, start=(n == 0), stop=(n == len(passes) - 1))
                    return ins_
                return go

            def three(w_h, w_l, x_h, x_l, tiles):
                out_ = []
                for k in range(tiles):
                    out_ += [(w_h(k), x_h(k)), (w_h(k), x_l(k)), (w_l(k), x_h(k))]
                return out_

            def project(b, what, t, weight=()):
                wi = "kvqu".index(what)
                j = t
                bk, free = next_bank()
                name = f"{what}{t}"
                rows = slice(t * P, (t + 1) * P)
                op("pe", products(bk[:, :], three(lambda k: w_hi[:, k, wi, rows], lambda k: w_lo[:, k, wi, rows],
                                                  lambda k: xn_hi[:, k, :], lambda k: xn_lo[:, k, :], KT)),
                   after=("xnT0 split", "xnT1 split", free) + weight, mark=f"{name} product")
                c.marks["projected"] = c.marks[f"{name} product"]
                op("act", lambda e: e.activation(pre[j][:, :], bk[:, :], ACT.Identity,
                                                 bias=vecs[:, 2 * wi + t:2 * wi + t + 1]),
                   after=(f"{name} product", f"pre{j} used") + weight, mark=f"{name} pre")
                c.marks[free] = c.marks[f"{name} pre"]
                dst = {"k": kT[b], "v": vT, "q": qT[b], "u": uT[b]}[what]
                if what in "kq":
                    op("act", lambda e: e.activation(act_out[j][:, :], pre[j][:, :], ACT.Exp),
                       after=(f"{name} pre",), mark=f"{name} exp")
                    op("dve", lambda e: e.tensor_scalar(pre[j][:, :], pre[j][:, :], -1.0, -1.0, ALU.add, ALU.max),
                       after=(f"{name} exp",), mark=f"{name} linear")
                    op("dve", lambda e: e.scalar_tensor_tensor(dst[:, t, :], act_out[j][:, :], 1.0, pre[j][:, :],
                                                               ALU.min, ALU.add),
                       after=(f"{name} linear",) + ((f"heads",) if what == "q" else ()), mark=f"{name} ready{b}")
                else:
                    op("act", lambda e: e.activation(act_out[j][:, :], pre[j][:, :], ACT.Tanh, scale=0.5),
                       after=(f"{name} pre",), mark=f"{name} tanh")
                    op("dve", lambda e: e.scalar_tensor_tensor(dst[:, t, :], act_out[j][:, :], 1.0, pre[j][:, :],
                                                               ALU.add, ALU.mult),
                       after=(f"{name} tanh",) + (("v in tokens",) if what == "v" else ()), mark=f"{name} ready{b}")
                c.marks[f"pre{j} used"] = c.marks[f"{name} ready{b}"]

            def spread_heads(b, after=()):
                def go(e):
                    return [e.dma_start(q_heads[DH * n:DH * (n + 1), :, n, :], qT[b][DH * n:DH * (n + 1), :, :])
                            for n in range(HPG)]
                dma("sp", "heads", go, after=(f"q0 ready{b}", f"q1 ready{b}", "scores") + after, n=HPG)

            def gate_logits(weight=()):
                bk, free = next_bank()
                op("pe", products(bk[:, :], [(wg[:, k, :], x[:, k, :]) for k in range(KT) for x in (xn_hi, xn_lo)]),
                   after=("xnT0 split", "xnT1 split", free) + weight, mark="logits")
                c.marks["projected"] = c.marks["logits"]
                op("act", lambda e: e.activation(logit_T[:, :], bk[:, :], ACT.Copy),
                   after=("logits", "logits in tokens"), mark="logit_T")
                c.marks[free] = c.marks["logit_T"]

            def choose_expert():
                bk, free = next_bank()
                parts = bk[:, :].rearrange("p (c n) -> p c n", c=CH)
                lt = logit[:, :, :]

                def go(e):
                    for k in range(CH):
                        last = e.transpose(bk[:, k * P:(k + 1) * P], logit_T[:, k * P:(k + 1) * P], ident[:, :])
                    return last
                op("pe", go, after=("logit_T", free), mark="logits in tokens")
                wide = [P, CH, NE]
                op("dve", lambda e: e.tensor_copy(lt, parts[:, :, NE_LO:NE_LO + NE]), after=("logits in tokens",),
                   mark="logit lo")
                op("dve", lambda e: e.tensor_tensor(lt, parts[:, :, 0:NE], lt, ALU.add), after=("logit lo",),
                   mark="logit")
                c.marks[free] = c.marks["logit"]
                op("dve", lambda e: e.tensor_reduce(top[:, :], lt, AX.X, ALU.max), after=("logit",), mark="top")
                op("dve", lambda e: e.tensor_tensor(hit[:, :, :], lt, top[:, :].unsqueeze(2).to_broadcast(wide),
                                                    ALU.is_equal), after=("top",), mark="hit")
                op("dve", lambda e: e.tensor_tensor(hit[:, :, :], hit[:, :, :], rank[:, :, :], ALU.mult),
                   after=("hit",), mark="ranked")
                op("dve", lambda e: e.tensor_reduce(win[:, :], hit[:, :, :], AX.X, ALU.max), after=("ranked",),
                   mark="win")
                for col in (0, NE_LO):
                    op("dve", lambda e, col=col: e.tensor_tensor(
                        onehot[:, :, col:col + NE], hit[:, :, :], win[:, :].unsqueeze(2).to_broadcast(wide),
                        ALU.is_equal), after=("win", "onehot transposed"), mark="onehot")

            def gate_rows(b):
                bk, free = next_bank()

                def go(e):
                    for k in range(CH):
                        last = e.transpose(bk[:, k * P:(k + 1) * P], onehot[:, k, :], ident[:, :])
                    return last
                op("pe", go, after=("onehot", free), mark="onehot transposed")
                op("dve", lambda e: e.tensor_scalar(off_T[b][0:NE, :], bk[0:NE, :], -1.0, 1.0, ALU.mult, ALU.add),
                   after=("onehot transposed", "hidden products"), mark="off_T")
                op("dve", lambda e: e.tensor_copy(on_T[b][:, :], bk[:, :]),
                   after=(f"expert products{b}",), mark="on_T")
                c.marks[free] = c.marks["on_T"]

            def to_tokens(src, dst, what, half, ready, dst_free):
                bk, free = next_bank()

                def go(e):
                    for k in (0, 1):
                        for t in range(KT):
                            col = k * D + t * P
                            tok = (2 * half + k) * P
                            last = e.transpose(bk[:, col:col + P], src[:, t, tok:tok + P], ident[:, :])
                    return last
                name = f"{what} T{half}"
                op("pe", go, after=ready + (free,), mark=name)
                c.marks[f"{what} in tokens"] = c.marks[name]
                op("act", lambda e: e.activation(dst[:, 2 * half:2 * half + 2, :].rearrange("p c d -> p (c d)"),
                                                 bk[:, :], ACT.Copy), after=(name,) + dst_free,
                   mark=f"{what}_tok{half}")
                c.marks[free] = c.marks[f"{what}_tok{half}"]

            def scores(b, k):
                for t in range(KT):
                    op("pe", lambda e, t=t: e.matmul(
                        e_bank[t][:, :].rearrange("p (h n) -> p h n", h=HPG),
                        kT[b][:, t, k * P:(k + 1) * P], q_heads[:, t, :, k * P:(k + 1) * P], start=True, stop=True),
                       after=("heads", f"k{t} ready{b}", f"energy{t} masked"), mark=f"scores{t}")
                    op("dve", lambda e, t=t: e.tensor_tensor(
                        energy[k % 2][:, t, :], e_bank[t][:, :], causal[:, :, :].rearrange("p h n -> p (h n)"),
                        ALU.mult), after=(f"scores{t}", f"attended{k % 2}"), mark=f"energy{t} masked")
                c.marks["scores"] = c.marks["scores1"]

            def attend(b, k):
                for t in range(KT):
                    def go(e, t=t):
                        tok = slice(k * P, (k + 1) * P)
                        e.matmul(o_bank[t][:, tok], state[b][:, t * P:(t + 1) * P], qT[b][:, t, tok],
                                 start=True, stop=False, skip_group_check=True)
                        for n in range(HPG):
                            last = e.matmul(o_bank[t][DH * n:DH * (n + 1), tok],
                                            v_tok[:, k, t * P + DH * n:t * P + DH * (n + 1)],
                                            energy[k % 2][:, t, P * n:P * (n + 1)],
                                            start=False, stop=True, skip_group_check=True,
                                            tile_position=(0, DH * n))
                        return last
                    op("pe", go, after=(f"energy{t} masked", f"state{b}", "v_tok0", "v_tok1", f"att{t} read"),
                       mark=f"att{t}")
                c.marks[f"attended{k % 2}"] = c.marks["att1"]

                def kv(e):
                    for t in range(KT):
                        cols = slice(t * P, (t + 1) * P)
                        last = e.matmul(kv_bank[:, cols], k_tok[:, k, cols], v_tok[:, k, cols],
                                        start=True, stop=True)
                    return last
                op("pe", kv, after=("k_tok0", "k_tok1", "kv masked"), mark="kv")
                op("dve", lambda e: e.tensor_tensor(kv_new[:, :], kv_bank[:, 0:D],
                                                    diag[:, :, :].rearrange("p t n -> p (t n)"), ALU.mult),
                   after=("kv", f"state{b}"), mark="kv masked")
                op("dve", lambda e: e.tensor_tensor(state[b][:, :], state[b][:, :], kv_new[:, :], ALU.add),
                   after=("kv masked", "att1"), mark=f"state{b}")

            def attention_out(b):
                for t in range(KT):
                    op("act", lambda e, t=t: e.activation(sq[:, t, :], o_bank[t][:, :], ACT.Square),
                       after=(f"att{t}", "ya in tokens"), mark=f"sq{t}")
                    op("dve", lambda e, t=t: e.tensor_tensor(g[:, t, :], o_bank[t][:, :], uT[b][:, t, :], ALU.mult),
                       after=(f"sq{t}", f"u{t} ready{b}", f"g{t} split"), mark=f"g{t}")
                    c.marks[f"att{t} read"] = c.marks[f"g{t}"]
                    if t == KT - 1:
                        op("pool", lambda e: e.tensor_tensor(sq[:, 0, :], sq[:, 0, :], sq[:, 1, :], ALU.add),
                           after=("sq0", "sq1"), mark="sq sum")
                    op("dve", lambda e, t=t: e.tensor_copy(g_hi[:, t, :], g[:, t, :]),
                       after=(f"g{t}", "wo products"), mark=f"g{t} hi")
                    op("pool", lambda e, t=t: e.tensor_tensor(g_lo[:, t, :], g[:, t, :], f32(g_hi[:, t, :]),
                                                              ALU.subtract),
                       after=(f"g{t} hi",), mark=f"g{t} split")

            def sum_squares():
                bk, free = next_bank()
                op("pe", products(bk[:, :], [(ones[:, :], sq[:, 0, :])]),
                   after=("sq sum", free), mark="ssq product")
                op("act", lambda e: e.activation(ssq[:, :], bk[:, :], ACT.Copy),
                   after=("ssq product", "ssq in tokens"), mark="ssq")
                c.marks[free] = c.marks["ssq"]

            def inverse_rms():
                bk, free = next_bank()

                def go(e):
                    for k in range(CH):
                        last = e.transpose(bk[:, k * P:(k + 1) * P], ssq[:, k * P:(k + 1) * P], ident[:, :])
                    return last
                op("pe", go, after=("ssq", free), mark="ssq in tokens")
                op("dve", lambda e: e.tensor_scalar(ms[:, :], bk[:, :].rearrange("p (c n) -> p c n", c=CH)[:, :, 0], 1.0 / D, None, ALU.mult),
                   after=("ssq in tokens",), mark="ms")
                c.marks[free] = c.marks["ms"]
                op("pool", lambda e: e.tensor_tensor(rms[:, :], ms[:, :], half_pow[:, :], ALU.pow),
                   after=("ms",), mark="rms")
                op("pool", lambda e: e.tensor_scalar(rms[:, :], rms[:, :], RMS_EPS, 1.0, ALU.add, ALU.mult),
                   after=("rms",), mark="rms eps", apart=True)
                op("dve", lambda e: e.reciprocal(rinv[:, :], rms[:, :]), after=("rms eps",), mark="rinv")

            def attention_product(t):
                bk, free = next_bank()
                cols = slice(t * P, (t + 1) * P)
                op("pe", products(bk[:, :], three(lambda k: wo_hi[:, k, cols], lambda k: wo_lo[:, k, cols],
                                                  lambda k: g_hi[:, k, :], lambda k: g_lo[:, k, :], KT)),
                   after=("g0 split", "g1 split", free), mark="wo products")
                op("act", lambda e: e.activation(ya[:, t, :], bk[:, :], ACT.Copy),
                   after=("wo products", "ssq product", "ya in tokens"), mark=f"ya{t}")
                c.marks[free] = c.marks[f"ya{t}"]

            def hidden(b, m):
                bk, free = next_bank()
                cols = slice(m * P, (m + 1) * P)
                j = m % 2
                op("pe", products(bk[:, :], three(lambda k: w1_hi[:, k, cols], lambda k: w1_lo[:, k, cols],
                                                  lambda k: xh_hi[:, k, :], lambda k: xh_lo[:, k, :], KT)
                                  + [(expert_off[:, 2 * m:2 * m + 2, :].rearrange("p e j -> p (e j)"),
                                      off_T[b][:, :])]),
                   after=("xhT0 split", "xhT1 split", "off_T", free), mark="hidden products")
                op("act", lambda e: e.activation(h[j][:, :], bk[:, :], ACT.Gelu, bias=h_bias[:, m:m + 1]),
                   after=("hidden products", f"h{j} split"), mark=f"h{j}")
                c.marks[free] = c.marks[f"h{j}"]
                op("dve", lambda e: e.tensor_copy(h_hi[:, m, :], h[j][:, :]),
                   after=(f"h{j}", "expert products"), mark=f"h{j} hi")
                op("pool", lambda e: e.tensor_tensor(h_lo[:, m, :], h[j][:, :], f32(h_hi[:, m, :]), ALU.subtract),
                   after=(f"h{j} hi",), mark=f"h{j} split")

            def expert_product(b, t):
                bk, free = next_bank()
                cols = slice(t * P, (t + 1) * P)
                op("pe", products(bk[:, :], [(b2[:, cols], on_T[b][:, :])]
                                  + three(lambda k: w2_hi[:, k, cols], lambda k: w2_lo[:, k, cols],
                                          lambda k: h_hi[:, k, :], lambda k: h_lo[:, k, :], MT)),
                   after=("on_T", "h0 split", "h1 split", free), mark="expert products")
                c.marks[f"expert products{b}"] = c.marks["expert products"]
                op("act", lambda e: e.activation(yf[:, t, :], bk[:, :], ACT.Identity, bias=vecs[:, 8 + t:9 + t]),
                   after=("expert products", "yf in tokens"), mark=f"yf{t}")
                c.marks[free] = c.marks[f"yf{t}"]

            def load_residual(i, b):
                dma("sp", "res", lambda e: [e.dma_start(x_res[:, :, :], x_steps[i, b])], after=("attention added",))

            def finish(i, b):
                for half in (0, 1):
                    bk, free = next_bank()

                    def tr(src):
                        def go(e):
                            for k in (0, 1):
                                for t in range(KT):
                                    tok = (2 * half + k) * P
                                    last = e.transpose(bk_[:, k * D + t * P:k * D + (t + 1) * P],
                                                       src[:, t, tok:tok + P], ident[:, :])
                            return last
                        return go
                    bk_ = bk
                    op("pe", tr(ya), after=("ya0", "ya1", free), mark="ya in tokens")

                    def add(e):
                        for k in (0, 1):
                            n = 2 * half + k
                            last = e.scalar_tensor_tensor(o[:, n, :], bk[:, k * D:(k + 1) * D], rinv[:, n:n + 1],
                                                          x_res[:, n, :], ALU.mult, ALU.add)
                        return last
                    op("dve", add, after=("ya in tokens", "rinv", "res", "store"), mark="attention added")
                    c.marks[free] = c.marks["attention added"]
                for half in (0, 1):
                    bk, free = next_bank()
                    bk_ = bk
                    op("pe", tr_at(yf, bk, half), after=("yf0", "yf1", free), mark="yf in tokens")
                    both = slice(2 * half, 2 * half + 2)
                    op("dve", lambda e: e.tensor_tensor(o[:, both, :].rearrange("p c d -> p (c d)"),
                                                        o[:, both, :].rearrange("p c d -> p (c d)"), bk[:, :],
                                                        ALU.add),
                       after=("yf in tokens", "attention added"), mark="o")
                    c.marks[free] = c.marks["o"]
                dma("sp", "store", lambda e: [e.dma_start(out_steps[i, b], o[:, :, :])], after=("o",))

            def tr_at(src, bk, half):
                def go(e):
                    for k in (0, 1):
                        for t in range(KT):
                            tok = (2 * half + k) * P
                            last = e.transpose(bk[:, k * D + t * P:k * D + (t + 1) * P],
                                               src[:, t, tok:tok + P], ident[:, :])
                    return last
                return go

            def constants():
                op("pool", lambda e: e.memset(ident[:, :], 0.0), mark="ident 0")
                op("pool", lambda e: e.affine_select(out=ident[:, :], in_=ident[:, :], compare_op=ALU.not_equal,
                                                     fill=1.0, base=0, pattern=[[-1, P]], channel_multiplier=1),
                   after=("ident 0",), mark="ident")
                op("pool", lambda e: e.memset(causal[:, :, :], 0.5), mark="causal 0")
                op("pool", lambda e: e.affine_select(out=causal[:, :, :], in_=causal[:, :, :], compare_op=ALU.is_ge,
                                                     fill=0.0, base=0, pattern=[[0, HPG], [1, P]],
                                                     channel_multiplier=-1),
                   after=("causal 0",), mark="causal")
                op("pool", lambda e: e.memset(expert_off[:, :, :], OFF), mark="expert_off 0")
                op("pool", lambda e: e.affine_select(out=expert_off[:, :, :], in_=expert_off[:, :, :],
                                                     compare_op=ALU.is_equal, fill=0.0, base=0,
                                                     pattern=[[-1, NE], [0, HE]], channel_multiplier=1),
                   after=("expert_off 0",), mark="expert_off")
                op("pool", lambda e: e.memset(half_pow[:, :], 0.5))
                op("pool", lambda e: e.memset(inv_half_pow[:, :], -0.5), mark="powers")

                def zeros(e):
                    e.memset(diag[:, :, :], 0.0)
                    e.memset(ones[:, :], 1.0)
                    for n in range(NE):
                        e.memset(rank[:, :, n:n + 1], float(NE - n))
                    for b in (0, 1):
                        e.memset(state[b][:, :], 0.0)
                        e.memset(off_T[b][:, :], 0.0)
                        e.memset(f32(on_T[b][:, :]), 0.0)
                    e.memset(f32(wg[:, :, :]), 0.0)
                    e.memset(onehot[:, :, :], 0.0)
                    return e.memset(f32(b2[:, :]), 0.0)
                op("dve", zeros, mark="zeros")
                for b in (0, 1):
                    c.marks[f"state{b}"] = c.marks["zeros"]

                def blocks(e):
                    for n in range(HPG):
                        last = e.memset(diag[DH * n:DH * (n + 1), :, DH * n:DH * (n + 1)], 0.5)
                    return last
                op("dve", blocks, after=("zeros",), mark="diag")

            def load_weights():
                dma("act", "w_small", lambda e: [e.dma_start(cols[:, :], ins["cols"])]
                    + [e.dma_start(b2_raw[row:row + NE, :], ins["b2"]) for row in (0, NE_LO)], n=3)
                load_x(0, 0)
                for wi, what in enumerate("kvqu"):
                    dma("sp", f"w_{what}", lambda e, what=what, wi=wi: [e.dma_start(w_raw[what], ins["w_in"][wi])])
                load_x(0, 1)
                dma("sp", "w_1", lambda e: [e.dma_start(w1_raw, ins["w_1"])])
                dma("sp", "w_2", lambda e: [e.dma_start(w2_raw, ins["w_2"])])
                dma("sp", "w_o", lambda e: [e.dma_start(wo_raw, ins["w_o"])])

            def small_weights():
                op("dve", lambda e: e.tensor_copy(wg[:, :, 0:NE], wg_cols), after=("zeros", "w_small"), mark="wg hi")
                for row in (0, NE_LO):
                    op("dve", lambda e, row=row: e.tensor_copy(b2[row:row + NE, :], b2_raw[row:row + NE, :]),
                       mark="b2 hi")
                op("dve", lambda e: e.tensor_tensor(wg[:, :, NE_LO:NE_LO + NE], wg_cols, f32(wg[:, :, 0:NE]),
                                                    ALU.subtract), after=("wg hi",), mark="wg")
                lo = slice(NE_LO, NE_LO + NE)
                op("dve", lambda e: e.tensor_tensor(b2[lo, :], b2_raw[lo, :], f32(b2[lo, :]), ALU.subtract),
                   after=("b2 hi",), mark="b2")

            def input_weight(what, who="dve"):
                wi = "kvqu".index(what)
                raw = w_raw[what].rearrange("p (k e) -> p k e", k=KT)
                split(w_hi[:, :, wi, :], w_lo[:, :, wi, :], raw, (f"w_{what}",), None, f"W{what}", who=who)

            def expert_weights():
                raw1 = w1_raw.rearrange("p (k n) -> p k n", k=KT)
                for k in range(KT):
                    op("dve", lambda e, k=k: e.tensor_tensor(
                        w1_sc[:, k, :].rearrange("p (x j) -> p x j", x=NE),
                        raw1[:, k, :].rearrange("p (x j) -> p x j", x=NE),
                        ln_cols[:, 0, k, :].unsqueeze(2).to_broadcast([P, NE, HE]), ALU.mult),
                       after=("w_small", "w_1"), mark=f"W1{k} scaled")
                    split(w1_hi[:, k, :], w1_lo[:, k, :], w1_sc[:, k, :], (f"W1{k} scaled",), None, f"W1{k}", "dve", "pool")
                bk, free = next_bank()

                def go(e):
                    for m in range(MT):
                        for k in range(KT):
                            last = e.matmul(bk[:, 2 * m:2 * m + 2], raw1[:, k, m * P:(m + 1) * P],
                                            ln_cols[:, 1, k, 2 * m:2 * m + 2], start=(k == 0), stop=(k == KT - 1))
                    return last
                op("pe", go, after=("w_small", "w_1", free), mark="ln_bias product")
                pairs = bk[:, 0:2 * MT].rearrange("p (m x) -> p m x", x=2)
                for x in (0, 1):
                    rows = slice(HE * x, HE * (x + 1))
                    op("dve", lambda e, x=x, rows=rows: e.tensor_tensor(
                        h_bias[rows, :], pairs[rows, :, x], vecs[rows, 12:16], ALU.add),
                       after=("ln_bias product",), mark="h_bias")
                c.marks[free] = c.marks["h_bias"]

            def output_weights():
                for k in range(KT):
                    op("dve", lambda e, k=k: e.tensor_scalar(wo_sc[:, k * D:(k + 1) * D], wo_raw[:, k * D:(k + 1) * D],
                                                             vecs[:, 10 + k:11 + k], 0.5, ALU.mult, ALU.mult),
                       after=("w_o", "w_small"), mark="Wo scaled")
                split(wo_hi[:, :, :], wo_lo[:, :, :], wo_sc[:, :].rearrange("p (k e) -> p k e", k=KT),
                      ("Wo scaled",), None, "Wo", "dve", "pool")
                split(w2_hi[:, :, :], w2_lo[:, :, :], w2_raw.rearrange("p (m d) -> p m d", m=MT), ("w_2",), None,
                      "W2", "dve", "pool")

            def tick(i, b, project_next=True, norm_next=True):
                n = 1 - b
                turn[0] = 0
                ni = i + b
                units = [(w, t) for w in "kvqu" for t in range(KT)]
                load_residual(i, b)
                if norm_next:
                    load_x(i + 1, b)
                for k in range(CH):
                    scores(b, k)
                    if project_next:
                        for w, t in units[2 * k:2 * k + 2]:
                            project(n, w, t)
                    attend(b, k)
                    if k == 0 and norm_next:
                        norm_x(b)
                    if k == 2 and norm_next:
                        norm_again(b)
                if project_next:
                    gate_logits()
                    spread_heads(n)
                attention_out(b)
                hidden(b, 0)
                hidden(b, 1)
                if norm_next:
                    transpose_xn(0)
                    transpose_xn(1)
                sum_squares()
                hidden(b, 2)
                hidden(b, 3)
                if project_next:
                    choose_expert()
                attention_product(0)
                attention_product(1)
                inverse_rms()
                if project_next:
                    for half in (0, 1):
                        to_tokens(kT[n], k_tok, "k", half, (f"k0 ready{n}", f"k1 ready{n}"), ("kv",))
                    for half in (0, 1):
                        to_tokens(vT, v_tok, "v", half, (f"v0 ready{n}", f"v1 ready{n}"), ("kv",))
                    transpose_xh(n, 0)
                    transpose_xh(n, 1)
                expert_product(b, 0)
                expert_product(b, 1)
                if project_next:
                    gate_rows(n)
                finish(i, b)

            c.op("act", lambda e: e.preload_act_table(ACT.Exp))
            constants()
            load_weights()
            norm_x(0, "dve", meanwhile=lambda: input_weight("k"))
            transpose_xn(0)
            transpose_xn(1)
            for what in "vqu":
                input_weight(what, "pool")
            norm_again(0, "dve")
            small_weights()
            op("pool", lambda e: e.memset(q_heads[:, :, :, :], 0.0), mark="q_heads 0")
            for w in "kvqu":
                for t in range(KT):
                    project(0, w, t, (f"W{w} split", "w_small"))
                if w == "k":
                    output_weights()
                if w == "v":
                    norm_x(1)
                if w == "q":
                    expert_weights()
            gate_logits(("wg",))
            spread_heads(0, ("q_heads 0",))
            transpose_xh(0, 0)
            transpose_xh(0, 1)
            norm_again(1, "dve", meanwhile=choose_expert)
            for half in (0, 1):
                to_tokens(kT[0], k_tok, "k", half, ("k0 ready0", "k1 ready0"), ())
            for half in (0, 1):
                to_tokens(vT, v_tok, "v", half, ("v0 ready0", "v1 ready0"), ())
            gate_rows(0)
            transpose_xn(0)
            transpose_xn(1)

            pairs = STEPS // 2

            def body():
                tick(c.i if c.i is not None else 0, 0)
                tick(c.i if c.i is not None else 0, 1)
            c.loop(pairs - 1, body)
            tick(pairs - 1, 0, norm_next=False)
            tick(pairs - 1, 1, project_next=False, norm_next=False)
            if c.me == "sp":
                c.wait("store")

        dry = Counts(None, None, sems)
        schedule(dry)
        body = dry.found
        walks = {}
        for me in list(ENGINES) + ["sp"]:
            walks[me] = body
        uses = list(sems)

        block = ctx.enter_context(nc.Block())

        def run(me, eng):
            c = Counts(me, eng, sems, body)
            c.uses = uses
            c.apart = apart
            schedule(c)

        @block.tensor
        def _(eng):
            run("pe", eng)

        @block.scalar
        def _(eng):
            run("act", eng)

        @block.vector
        def _(eng):
            run("dve", eng)

        @block.gpsimd
        def _(eng):
            run("pool", eng)

        @block.sync
        def _(eng):
            run("sp", eng)


def kernel(**inputs):
    import numpy as np
    import concourse.bacc as bacc
    from concourse.bass_utils import run_bass_kernel_spmd

    nc = bacc.Bacc("TRN2", target_bir_lowering=False, num_devices=1)
    a = {name.replace("L0_attn_", "").replace("L0_ffn_", ""): np.asarray(v) for name, v in inputs.items()}

    def by_feature(w):
        return w.T.reshape(KT, P, -1).transpose(1, 0, 2)

    vecs = np.concatenate([a[n].reshape(-1) for n in ("bk", "bv", "bq", "bu", "bo", "scale", "b1")]).reshape(16, P)
    laid = {
        "x": a["x"],
        "w_in": np.stack([by_feature(a[f"W{n}"]).reshape(P, -1) for n in "kvqu"]),
        "w_o": by_feature(a["Wo"]).reshape(P, -1),
        "w_1": by_feature(a["W1"].transpose(0, 2, 1).reshape(NE * HE, D)).reshape(P, -1),
        "w_2": a["W2"].reshape(MT, P, D).transpose(1, 0, 2).reshape(P, -1),
        "b2": a["b2"],
        "cols": np.concatenate([vecs.T] + [by_feature(a[n]).reshape(P, -1) for n in ("ln_scale", "ln_bias", "Wg")],
                               axis=1),
    }
    arrays, ins = {}, {}
    for name, value in laid.items():
        arrays[f"in_{name}"] = np.ascontiguousarray(value)
        ins[name] = nc.dram_tensor(f"in_{name}", value.shape, mybir.dt.from_np(value.dtype),
                                   kind="ExternalInput").ap()
    out = nc.dram_tensor("out", (B, T, D), F32, kind="ExternalOutput").ap()
    build(nc, ins, out)
    result = run_bass_kernel_spmd(nc, [arrays], core_ids=[0])
    return result.results[0]["out"]
```

```python
import concourse.bass as bass
from concourse import mybir
from contextlib import ExitStack

F32 = mybir.dt.float32
F32R = mybir.dt.float32r
BF16 = mybir.dt.bfloat16
ALU = mybir.AluOpType
ACT = mybir.ActivationFunctionType
AX = mybir.AxisListType

B, T, D = 2, 2048, 256
HEADS, DH = 8, 32
NE, HE = 8, 64
NE_LO = 32
P = 128
CH = 4
NT = CH * P
STEPS = B * T // NT
KT = D // P
HPG = P // DH
MT = NE * HE // P
LN_EPS = 1e-5
RMS_EPS = 1e-8
OFF = -1e30

ENGINES = ("pe", "act", "dve", "pool")


class Counts:

    def __init__(self, me, eng, sems, body=None, apart=None):
        self.me, self.eng, self.sems = me, eng, sems
        self.body = body
        self.apart = apart
        self.count = {n: 0 for n in sems}
        self.start = {n: 0 for n in sems}
        self.marks = {}
        self.i = None
        self.waited = {}
        self.scaled = {}

    def value(self, sem, count):
        if self.i is None:
            return count
        return self.scaled[sem] + (self.start[sem] + count)

    def wait(self, *names, apart=False):
        issued = False
        for name in names:
            if name not in self.marks:
                continue
            sem, count = self.marks[name]
            if self.me and count > self.waited.get(sem, -10 ** 9):
                self.waited[sem] = count
                if self.i is not None or count > 0:
                    self.eng.wait_ge(self.sems[sem], self.value(sem, count))
                    issued = True
                    if self.me == "sp" and self.i is not None:
                        self.eng.sem_inc(self.apart["sp"], 1)
        if apart and issued and self.me != "sp" and self.i is not None:
            self.eng.sem_inc(self.apart[self.me], 1)

    def op(self, who, issue, after=(), mark=None, apart=False):
        ins = None
        if who == self.me:
            self.wait(*after, apart=apart)
            ins = issue(self.eng)
        if mark:
            if ins is not None:
                ins.then_inc(self.sems[who], 1)
            self.count[who] += 1
            self.marks[mark] = (who, self.count[who])

    def dma(self, who, sem, issue, after=(), n=1):
        if who == self.me:
            self.wait(*after, apart=True)
            for ins in issue(self.eng):
                ins.then_inc(self.sems[sem], 16)
        self.count[sem] += 16 * n
        self.marks[sem] = (sem, self.count[sem])

    def loop(self, times, body):
        per = {n: self.body["count"][n] if self.body else 0 for n in self.sems}
        if self.me in ENGINES:
            self.eng.drain().then_inc(self.sems[self.me], per[self.me])
        for n in self.sems:
            if n not in ENGINES and per[n] and self.me == "sp":
                self.eng.sem_inc(self.sems[n], per[n])
            self.count[n] += per[n]
            if n in ENGINES and self.me:
                self.eng.wait_ge(self.sems[n], self.count[n])
        self.start, before = dict(self.count), dict(self.count)
        self.count = {n: 0 for n in self.sems}
        if self.body:
            self.marks = {name: (sem, count - per[sem]) for name, (sem, count) in self.body["marks"].items()}
        if self.me:
            with self.eng.Fori(0, times) as i:
                self.i, self.waited = i, {}
                self.scaled = {n: self.eng.snap(i * per[n]) if per[n] else 0 for n in self.sems}
                body()
        else:
            body()
            self.found = {"count": dict(self.count), "marks": dict(self.marks)}
            per = self.count
        self.i, self.waited = None, {}
        last = {n: before[n] + (times - 1) * per[n] for n in self.sems}
        self.marks = {name: (sem, count + last[sem]) for name, (sem, count) in self.marks.items()}
        self.count = {n: before[n] + times * per[n] for n in self.sems}


def build(nc, ins, out):
    ctx = ExitStack()
    with ctx:
        def sb(name, shape, dt=F32):
            return ctx.enter_context(nc.sbuf_tensor(name, shape, dt))

        def bank(name):
            return ctx.enter_context(nc.psum_tensor(name, [P, 512], F32))

        ident = sb("ident", [P, P])
        causal = sb("causal", [P, P])
        half_pow = sb("half_pow", [P, CH])
        inv_half_pow = sb("inv_half_pow", [P, CH])
        rank = sb("rank", [P, CH, NE])
        expert_off = sb("expert_off", [P, NE, HE], BF16)
        w_hi = sb("w_hi", [P, KT, 4, D], F32R)
        w_lo = sb("w_lo", [P, KT, 4, D], F32R)
        wo_hi = sb("wo_hi", [P, KT, D], F32R)
        wo_lo = sb("wo_lo", [P, KT, D], F32R)
        w1_hi = sb("w1_hi", [P, KT, NE * HE], F32R)
        w1_lo = sb("w1_lo", [P, KT, NE * HE], F32R)
        w2_hi = sb("w2_hi", [P, MT, D], F32R)
        w2_lo = sb("w2_lo", [P, MT, D], F32R)
        wg = sb("wg", [P, KT, P], F32R)
        b2 = sb("b2", [P, D], F32R)
        cols = sb("cols", [P, 16 + 3 * KT * NE])
        vecs = cols[:, 0:16]
        ln_cols = cols[:, 16:16 + 2 * KT * NE].rearrange("p (w k e) -> p w k e", w=2, k=KT)
        wg_cols = cols[:, 16 + 2 * KT * NE:].rearrange("p (k e) -> p k e", k=KT)
        h_bias = sb("h_bias", [P, MT])
        x_in = [sb(f"x_in{b}", [P, CH, D]) for b in (0, 1)]
        xn = sb("xn", [P, CH, D])
        xn_hi = sb("xn_hi", [P, KT, NT], F32R)
        xn_lo = sb("xn_lo", [P, KT, NT], F32R)
        xh_hi = sb("xh_hi", [P, KT, NT], F32R)
        xh_lo = sb("xh_lo", [P, KT, NT], F32R)
        pre = [sb(f"pre{j}", [P, NT]) for j in (0, 1)]
        act_out = [sb(f"act_out{j}", [P, NT]) for j in (0, 1)]
        kT = sb("kT", [P, KT, NT])
        k_hi = sb("k_hi", [P, KT, NT], F32R)
        k_lo = sb("k_lo", [P, KT, NT], F32R)
        qT = [sb(f"qT{b}", [P, KT, NT]) for b in (0, 1)]
        uT = [sb(f"uT{b}", [P, KT, NT]) for b in (0, 1)]
        vT = sb("vT", [P, KT, NT])
        q_heads = [sb(f"q_heads_{part}", [P, KT, HPG, NT], F32R) for part in ("hi", "lo")]
        k_tok = sb("k_tok", [P, CH, D])
        v_tok = sb("v_tok", [P, CH, D])
        energy = [sb(f"energy{c}", [P, KT, 512]) for c in (0, 1)]
        state = [sb(f"state{b}", [P, D]) for b in (0, 1)]
        g = sb("g", [P, KT, NT])
        g_hi = sb("g_hi", [P, KT, NT], F32R)
        g_lo = sb("g_lo", [P, KT, NT], F32R)
        h = act_out
        h_hi = sb("h_hi", [P, MT, NT], F32R)
        h_lo = sb("h_lo", [P, MT, NT], F32R)
        ya = sb("ya", [P, KT, NT])
        yf = g
        q_split = [h_hi[:, 0:KT, :], h_lo[:, 0:KT, :]]
        sq = ya
        o = sb("o", [P, CH, D])
        off_T = [sb(f"off_T{b}", [P, NT], BF16) for b in (0, 1)]
        on_T = [sb(f"on_T{b}", [P, NT], F32R) for b in (0, 1)]
        logit_T = pre[1]
        onehot = sb("onehot", [P, CH, P])
        logit = sb("logit", [P, CH, NE])
        hit = sb("hit", [P, CH, NE])
        top = sb("top", [P, CH])
        win = sb("win", [P, CH])
        stats = [sb(f"stats{j}", [P, CH, 6]) for j in (0, 1)]
        mv = [sb(f"mv{j}", [P, CH, 2]) for j in (0, 1)]
        eps_var = [sb(f"eps_var{j}", [P, CH]) for j in (0, 1)]
        neg_mean = [sb(f"neg_mean{j}", [P, CH]) for j in (0, 1)]
        rstd = [sb(f"rstd{j}", [P, CH]) for j in (0, 1)]
        shift = [sb(f"shift{j}", [P, CH]) for j in (0, 1)]
        ssq = sb("ssq", [P, CH])
        ms = sb("ms", [P, CH])
        rms = sb("rms", [P, CH])
        rinv = sb("rinv", [P, CH])
        w_raw = {"k": energy[0][:, 0, :], "v": energy[0][:, 1, :], "q": energy[1][:, 0, :], "u": energy[1][:, 1, :]}
        w1_raw, w2_raw = ya[:, :, :], g[:, :, :].rearrange("p k n -> p (k n)")
        w1_sc = energy[0][:, :, :]
        wo_raw, wo_sc = o[:, 0:2, :].rearrange("p c d -> p (c d)"), o[:, 2:4, :].rearrange("p c d -> p (c d)")
        b2_raw = k_tok[:, 0, :]

        ring = [bank(f"ring{r}") for r in range(3)]
        e_bank = [bank(f"energy_bank{t}") for t in range(KT)]
        o_bank = [bank(f"att_bank{t}") for t in range(KT)]
        kv_bank = bank("kv_bank")
        kv_sum = [kv_bank[:, b * D:(b + 1) * D] for b in (0, 1)]

        dma_sems = ["w_k", "w_v", "w_q", "w_u", "w_o", "w_1", "w_2", "w_small", "x_even", "x_odd", "heads",
                    "res", "store"]
        sems = {n: ctx.enter_context(nc.semaphore(f"s_{n}")) for n in list(ENGINES) + dma_sems}

        apart = {n: ctx.enter_context(nc.semaphore(f"s_apart_{n}")) for n in ("dve", "pool", "sp")}

        x_steps = ins["x"].rearrange("b (i c p) d -> i b p c d", c=CH, p=P)
        out_steps = out.rearrange("b (i c p) d -> i b p c d", c=CH, p=P)

        def f32(ap):
            return ap.bitcast(F32)

        def schedule(c):
            op, dma = c.op, c.dma
            turn = {}
            banks = {"ring": [(ring[r], f"ring{r} free") for r in range(len(ring))],
                     "energy": [(e_bank[t], f"energy{t} masked") for t in range(KT)],
                     "attention": [(o_bank[t], f"att{t} read") for t in range(KT)]}

            def next_bank(kind="ring"):
                n = turn.get(kind, 0)
                turn[kind] = n + 1
                return banks[kind][n % len(banks[kind])]

            def split(dst_hi, dst_lo, src, after, free, name, who="dve"):
                op("act", lambda e: e.activation(dst_hi, src, ACT.Copy), after=after, mark=f"{name} hi")
                op(who, lambda e: e.tensor_tensor(dst_lo, src, f32(dst_hi), ALU.subtract),
                   after=(f"{name} hi",), mark=f"{name} split")
                if free:
                    c.marks[free] = c.marks[f"{name} split"]

            def load_x(i, b):
                dma("sp", ("x_even", "x_odd")[b], lambda e: [e.dma_start(x_in[b][:, :, :], x_steps[i, b])],
                    after=(f"xh{b} transposed",))

            def norm(b, j, src, dst, src_ready, dst_free, who, meanwhile=lambda: None):
                def stat(e):
                    for k in range(CH):
                        last = e.bn_stats(stats[j][:, k, :], src[:, k, :])
                    return last
                op("dve", stat, after=src_ready, mark=f"stats{j}")

                def aggr(e):
                    for k in range(CH):
                        last = e.bn_aggr(mv[j][:, k, :], stats[j][:, k, :])
                    return last
                op("dve", aggr, after=(f"stats{j}", f"norm{j} scalars"), mark=f"mv{j}", apart=True)
                op("pool", lambda e: e.tensor_scalar(eps_var[j][:, :], mv[j][:, :, 1], LN_EPS, 1.0, ALU.add, ALU.mult),
                   after=(f"mv{j}",), mark=f"eps_var{j}", apart=True)
                op("pool", lambda e: e.tensor_scalar(neg_mean[j][:, :], mv[j][:, :, 0], -1.0, 1.0, ALU.mult, ALU.mult),
                   mark=f"neg_mean{j}")
                op("pool", lambda e: e.tensor_tensor(rstd[j][:, :], eps_var[j][:, :], inv_half_pow[:, :], ALU.pow),
                   after=(f"eps_var{j}",), mark=f"rstd{j}")
                op("pool", lambda e: e.tensor_tensor(shift[j][:, :], neg_mean[j][:, :], rstd[j][:, :], ALU.mult),
                   after=(f"rstd{j}", f"neg_mean{j}"), mark=f"norm{j} scalars")

                meanwhile()

                def apply(e):
                    for k in range(CH):
                        last = e.tensor_scalar(dst[:, k, :], src[:, k, :], rstd[j][:, k:k + 1], shift[j][:, k:k + 1],
                                               ALU.mult, ALU.add)
                    return last
                op(who, apply, after=(f"norm{j} scalars",) + dst_free, mark=f"norm{j} done", apart=(who == "pool"))

            def norm_x(b, who="pool", **meanwhile):
                norm(b, 0, x_in[b], xn, (("x_even", "x_odd")[b],), ("xn transposed",), who, **meanwhile)

            def norm_again(b, who="pool", **meanwhile):
                norm(b, 1, xn, x_in[b], ("norm0 done",), (), who, **meanwhile)
                c.marks[f"xh{b} ready"] = c.marks["norm1 done"]

            def transpose_tokens(src, t, name, ready, kind="ring"):
                bk, free = next_bank(kind)

                def go(e):
                    for k in range(CH):
                        last = e.transpose(bk[:, k * P:(k + 1) * P], src[:, k, t * P:(t + 1) * P], ident[:, :])
                    return last
                op("pe", go, after=(ready, free), mark=name)
                return bk, free

            def transpose_xn(t):
                bk, free = transpose_tokens(xn, t, f"xn T{t}", "norm0 done", "attention")
                c.marks["xn transposed"] = c.marks[f"xn T{t}"]
                split(xn_hi[:, t, :], xn_lo[:, t, :], bk[:, :], (f"xn T{t}", "projected"), free, f"xnT{t}")

            def transpose_xh(b, t):
                bk, free = transpose_tokens(x_in[b], t, f"xh T{t}", f"xh{b} ready")
                c.marks[f"xh{b} transposed"] = c.marks[f"xh T{t}"]
                split(xh_hi[:, t, :], xh_lo[:, t, :], bk[:, :], (f"xh T{t}", "hidden products"), free, f"xhT{t}")

            def products(bk, passes):
                def go(e):
                    for n, (w, x) in enumerate(passes):
                        ins_ = e.matmul(bk, w, x, start=(n == 0), stop=(n == len(passes) - 1))
                    return ins_
                return go

            def three(w_h, w_l, x_h, x_l, tiles):
                out_ = []
                for k in range(tiles):
                    out_ += [(w_h(k), x_h(k)), (w_h(k), x_l(k)), (w_l(k), x_h(k))]
                return out_

            def project(b, what, t, weight=()):
                wi = "kvqu".index(what)
                j = t
                bk, free = next_bank()
                name = f"{what}{t}"
                rows = slice(t * P, (t + 1) * P)
                op("pe", products(bk[:, :], three(lambda k: w_hi[:, k, wi, rows], lambda k: w_lo[:, k, wi, rows],
                                                  lambda k: xn_hi[:, k, :], lambda k: xn_lo[:, k, :], KT)),
                   after=("xnT0 split", "xnT1 split", free) + weight, mark=f"{name} product")
                c.marks["projected"] = c.marks[f"{name} product"]
                op("act", lambda e: e.activation(pre[j][:, :], bk[:, :], ACT.Identity,
                                                 bias=vecs[:, 2 * wi + t:2 * wi + t + 1]),
                   after=(f"{name} product", f"pre{j} used") + (("logits in tokens",) if j else ()) + weight,
                   mark=f"{name} pre")
                c.marks[free] = c.marks[f"{name} pre"]
                dst = {"k": kT, "v": vT, "q": qT[b], "u": uT[b]}[what]
                dst_free = {"k": ("k in tokens", "k split"), "v": ("v in tokens",), "q": (), "u": ()}[what]
                if what in "kq":
                    op("act", lambda e: e.activation(act_out[j][:, :], pre[j][:, :], ACT.Exp),
                       after=(f"{name} pre", f"h{j} split"), mark=f"{name} exp")
                    op("dve", lambda e: e.tensor_scalar(pre[j][:, :], pre[j][:, :], -1.0, -1.0, ALU.add, ALU.max),
                       after=(f"{name} exp",), mark=f"{name} linear")
                    op("dve", lambda e: e.scalar_tensor_tensor(dst[:, t, :], act_out[j][:, :], 1.0, pre[j][:, :],
                                                               ALU.min, ALU.add),
                       after=(f"{name} linear",) + dst_free, mark=f"{name} ready{b}")
                    if what == "q":
                        hi, lo = q_split
                        op("dve", lambda e: e.tensor_copy(hi[:, t, :], dst[:, t, :]),
                           after=(f"{name} ready{b}", "expert products"), mark=f"{name} hi")
                        op("pool", lambda e: e.tensor_tensor(lo[:, t, :], dst[:, t, :], f32(hi[:, t, :]),
                                                             ALU.subtract), after=(f"{name} hi",),
                           mark=f"{name} split")
                else:
                    op("act", lambda e: e.activation(act_out[j][:, :], pre[j][:, :], ACT.Tanh, scale=0.5),
                       after=(f"{name} pre", f"h{j} split"), mark=f"{name} tanh")
                    op("dve", lambda e: e.scalar_tensor_tensor(dst[:, t, :], act_out[j][:, :], 1.0, pre[j][:, :],
                                                               ALU.add, ALU.mult),
                       after=(f"{name} tanh",) + dst_free, mark=f"{name} ready{b}")
                c.marks[f"pre{j} used"] = c.marks[f"{name} ready{b}"]

            def spread_heads(b, after=()):
                def go(e):
                    return [e.dma_start(f32(q_heads[part][DH * n:DH * (n + 1), :, n, :]),
                                        f32(q_split[part][DH * n:DH * (n + 1), :, :]))
                            for part in (0, 1) for n in range(HPG)]
                dma("sp", "heads", go, after=("q0 split", "q1 split", "scores") + after, n=2 * HPG)

            def split_keys(b):
                for t in range(KT):
                    op("dve", lambda e, t=t: e.tensor_copy(k_hi[:, t, :], kT[:, t, :]),
                       after=(f"k{t} ready{b}", "scores"), mark=f"k{t} hi")
                for t in range(KT):
                    op("pool", lambda e, t=t: e.tensor_tensor(k_lo[:, t, :], kT[:, t, :], f32(k_hi[:, t, :]),
                                                              ALU.subtract), after=(f"k{t} hi",), mark="k split")

            def gate_logits(weight=()):
                bk, free = next_bank()
                op("pe", products(bk[:, :], [(wg[:, k, :], x[:, k, :]) for k in range(KT) for x in (xn_hi, xn_lo)]),
                   after=("xnT0 split", "xnT1 split", free) + weight, mark="logits")
                c.marks["projected"] = c.marks["logits"]
                op("act", lambda e: e.activation(logit_T[:, :], bk[:, :], ACT.Copy),
                   after=("logits", "pre1 used"), mark="logit_T")
                c.marks[free] = c.marks["logit_T"]

            def choose_expert():
                bk, free = next_bank("energy")
                parts = bk[:, :].rearrange("p (c n) -> p c n", c=CH)
                lt = logit[:, :, :]

                def go(e):
                    for k in range(CH):
                        last = e.transpose(bk[:, k * P:(k + 1) * P], logit_T[:, k * P:(k + 1) * P], ident[:, :])
                    return last
                op("pe", go, after=("logit_T", free), mark="logits in tokens")
                wide = [P, CH, NE]
                op("dve", lambda e: e.tensor_copy(lt, parts[:, :, NE_LO:NE_LO + NE]), after=("logits in tokens",),
                   mark="logit lo")
                op("dve", lambda e: e.tensor_tensor(lt, parts[:, :, 0:NE], lt, ALU.add), after=("logit lo",),
                   mark="logit")
                c.marks[free] = c.marks["logit"]
                op("dve", lambda e: e.tensor_reduce(top[:, :], lt, AX.X, ALU.max), after=("logit",), mark="top")
                op("dve", lambda e: e.tensor_tensor(hit[:, :, :], lt, top[:, :].unsqueeze(2).to_broadcast(wide),
                                                    ALU.is_equal), after=("top",), mark="hit")
                op("dve", lambda e: e.tensor_tensor(hit[:, :, :], hit[:, :, :], rank[:, :, :], ALU.mult),
                   after=("hit",), mark="ranked")
                op("dve", lambda e: e.tensor_reduce(win[:, :], hit[:, :, :], AX.X, ALU.max), after=("ranked",),
                   mark="win")
                for col in (0, NE_LO):
                    op("dve", lambda e, col=col: e.tensor_tensor(
                        onehot[:, :, col:col + NE], hit[:, :, :], win[:, :].unsqueeze(2).to_broadcast(wide),
                        ALU.is_equal), after=("win", "onehot transposed"), mark="onehot")

            def gate_rows(b):
                bk, free = next_bank("energy")

                def go(e):
                    for k in range(CH):
                        last = e.transpose(bk[:, k * P:(k + 1) * P], onehot[:, k, :], ident[:, :])
                    return last
                op("pe", go, after=("onehot", free), mark="onehot transposed")
                op("dve", lambda e: e.tensor_scalar(off_T[b][0:NE, :], bk[0:NE, :], -1.0, 1.0, ALU.mult, ALU.add),
                   after=("onehot transposed", "hidden products"), mark=f"off_T{b}")
                op("dve", lambda e: e.tensor_copy(on_T[b][:, :], bk[:, :]),
                   after=(f"expert products{b}",), mark=f"on_T{b}")
                c.marks[free] = c.marks[f"on_T{b}"]

            def to_tokens(src, dst, what, half, ready, dst_free):
                bk, free = next_bank("attention")

                def go(e):
                    for k in (0, 1):
                        for t in range(KT):
                            col = k * D + t * P
                            tok = (2 * half + k) * P
                            last = e.transpose(bk[:, col:col + P], src[:, t, tok:tok + P], ident[:, :])
                    return last
                name = f"{what} T{half}"
                op("pe", go, after=ready + (free,), mark=name)
                c.marks[f"{what} in tokens"] = c.marks[name]
                op("act", lambda e: e.activation(dst[:, 2 * half:2 * half + 2, :].rearrange("p c d -> p (c d)"),
                                                 bk[:, :], ACT.Copy), after=(name,) + dst_free,
                   mark=f"{what}_tok{half}")
                c.marks[free] = c.marks[f"{what}_tok{half}"]

            def k_tokens(b, half):
                to_tokens(kT, k_tok, "k", half, (f"k0 ready{b}", f"k1 ready{b}"), ("kv",))

            def v_tokens(b, half):
                to_tokens(vT, v_tok, "v", half, (f"v0 ready{b}", f"v1 ready{b}"), ("kv",))

            def scores(b, k):
                for t in range(KT):
                    tok = slice(k * P, (k + 1) * P)
                    q_h, q_l = (part[:, t, :, tok] for part in q_heads)
                    op("pe", products(e_bank[t][:, :].rearrange("p (h n) -> p h n", h=HPG),
                                      [(k_hi[:, t, tok], q_h), (k_hi[:, t, tok], q_l), (k_lo[:, t, tok], q_h)]),
                       after=("heads", "k split", f"energy{t} masked"), mark=f"scores{t}")
                    op("dve", lambda e, t=t: e.tensor_tensor(
                        energy[k % 2][:, t, :].rearrange("p (h n) -> p h n", h=HPG),
                        e_bank[t][:, :].rearrange("p (h n) -> p h n", h=HPG),
                        causal[:, :].unsqueeze(1).to_broadcast([P, HPG, P]), ALU.mult),
                       after=(f"scores{t}", f"attended{k % 2}"), mark=f"energy{t} masked")
                c.marks["scores"] = c.marks["scores1"]

            def attend(b, k):
                tok = slice(k * P, (k + 1) * P)

                def before(e):
                    for t in range(KT):
                        last = e.matmul(o_bank[t][:, tok], state[b][:, t * P:(t + 1) * P], qT[b][:, t, tok],
                                        start=True, stop=False, skip_group_check=True)
                    return last
                op("pe", before, after=(f"state{b}", "att0 read", "att1 read"), mark="att before")
                for t in range(KT):
                    def inside(e, t=t):
                        for n in range(HPG):
                            last = e.matmul(o_bank[t][DH * n:DH * (n + 1), tok],
                                            v_tok[:, k, t * P + DH * n:t * P + DH * (n + 1)],
                                            energy[k % 2][:, t, P * n:P * (n + 1)],
                                            start=False, stop=True, skip_group_check=True,
                                            tile_position=(0, DH * n))
                        return last
                    op("pe", inside, after=(f"energy{t} masked", "v_tok0", "v_tok1"), mark=f"att{t}")
                c.marks[f"attended{k % 2}"] = c.marks["att1"]

                def kv(e):
                    for t in range(KT):
                        for n in range(HPG):
                            head = slice(t * P + DH * n, t * P + DH * (n + 1))
                            last = e.matmul(kv_sum[b][DH * n:DH * (n + 1), head], k_tok[:, k, head], v_tok[:, k, head],
                                            start=False, stop=True, skip_group_check=True, tile_position=(0, DH * n))
                    return last
                op("pe", kv, after=("k_tok0", "k_tok1", f"state{b}"), mark="kv")
                op("dve", lambda e: e.tensor_scalar(state[b][:, :], kv_sum[b], 0.5, None, ALU.mult),
                   after=("kv", "att1"), mark=f"state{b}")

            def attention_out(b):
                for t in range(KT):
                    op("act", lambda e, t=t: e.activation(sq[:, t, :], o_bank[t][:, :], ACT.Square),
                       after=(f"att{t}", "ya in tokens"), mark=f"sq{t}")
                    op("dve", lambda e, t=t: e.tensor_tensor(g[:, t, :], o_bank[t][:, :], uT[b][:, t, :], ALU.mult),
                       after=(f"sq{t}", f"u{t} ready{b}", "yf in tokens"), mark=f"g{t}")
                    c.marks[f"att{t} read"] = c.marks[f"g{t}"]
                    if t == KT - 1:
                        op("pool", lambda e: e.tensor_tensor(sq[:, 0, :], sq[:, 0, :], sq[:, 1, :], ALU.add),
                           after=("sq0", "sq1"), mark="sq sum")
                    op("dve", lambda e, t=t: e.tensor_copy(g_hi[:, t, :], g[:, t, :]),
                       after=(f"g{t}", "wo products"), mark=f"g{t} hi")
                    op("pool", lambda e, t=t: e.tensor_tensor(g_lo[:, t, :], g[:, t, :], f32(g_hi[:, t, :]),
                                                              ALU.subtract),
                       after=(f"g{t} hi",), mark=f"g{t} split")

            def root_mean_square():
                bk, free = next_bank("energy")

                def go(e):
                    for k in range(CH):
                        last = e.transpose(bk[:, k * P:(k + 1) * P], sq[:, 0, k * P:(k + 1) * P], ident[:, :])
                    return last
                op("pe", go, after=("sq sum", free), mark="squares in tokens")
                op("dve", lambda e: e.tensor_reduce(ssq[:, :], bk[:, :].rearrange("p (c n) -> p c n", c=CH), AX.X,
                                                    ALU.add), after=("squares in tokens",), mark="ssq")
                c.marks[free] = c.marks["ssq"]
                op("dve", lambda e: e.tensor_scalar(ms[:, :], ssq[:, :], 1.0 / D, None, ALU.mult),
                   after=("ssq",), mark="ms")
                op("pool", lambda e: e.tensor_tensor(rms[:, :], ms[:, :], half_pow[:, :], ALU.pow),
                   after=("ms",), mark="rms")
                op("pool", lambda e: e.tensor_scalar(rms[:, :], rms[:, :], RMS_EPS, 1.0, ALU.add, ALU.mult),
                   after=("rms",), mark="rms eps", apart=True)

            def attention_product(t):
                bk, free = next_bank()
                cols = slice(t * P, (t + 1) * P)
                op("pe", products(bk[:, :], three(lambda k: wo_hi[:, k, cols], lambda k: wo_lo[:, k, cols],
                                                  lambda k: g_hi[:, k, :], lambda k: g_lo[:, k, :], KT)),
                   after=("g0 split", "g1 split", free), mark="wo products")
                op("act", lambda e: e.activation(ya[:, t, :], bk[:, :], ACT.Copy),
                   after=("wo products", "squares in tokens", "ya in tokens"), mark=f"ya{t}")
                c.marks[free] = c.marks[f"ya{t}"]

            def hidden(b, m, lo_on=None):
                bk, free = next_bank()
                cols = slice(m * P, (m + 1) * P)
                j = m % 2
                op("pe", products(bk[:, :], three(lambda k: w1_hi[:, k, cols], lambda k: w1_lo[:, k, cols],
                                                  lambda k: xh_hi[:, k, :], lambda k: xh_lo[:, k, :], KT)
                                  + [(expert_off[:, 2 * m:2 * m + 2, :].rearrange("p e j -> p (e j)"),
                                      off_T[b][:, :])]),
                   after=("xhT0 split", "xhT1 split", f"off_T{b}", free), mark="hidden products")
                op("act", lambda e: e.activation(h[j][:, :], bk[:, :], ACT.Gelu, bias=h_bias[:, m:m + 1]),
                   after=("hidden products", f"h{j} split", f"pre{j} used"), mark=f"h{j}")
                c.marks[free] = c.marks[f"h{j}"]
                op("dve", lambda e: e.tensor_copy(h_hi[:, m, :], h[j][:, :]),
                   after=(f"h{j}", "expert products", "heads"), mark=f"h{j} hi")
                op(lo_on or ("dve", "pool")[j],
                   lambda e: e.tensor_tensor(h_lo[:, m, :], h[j][:, :], f32(h_hi[:, m, :]), ALU.subtract),
                   after=(f"h{j} hi",), mark=f"h{j} split")

            def expert_product(b, t):
                bk, free = next_bank()
                cols = slice(t * P, (t + 1) * P)
                op("pe", products(bk[:, :], [(b2[:, cols], on_T[b][:, :])]
                                  + three(lambda k: w2_hi[:, k, cols], lambda k: w2_lo[:, k, cols],
                                          lambda k: h_hi[:, k, :], lambda k: h_lo[:, k, :], MT)),
                   after=(f"on_T{b}", "h0 split", "h1 split", free), mark="expert products")
                c.marks[f"expert products{b}"] = c.marks["expert products"]
                op("act", lambda e: e.activation(yf[:, t, :], bk[:, :], ACT.Identity, bias=vecs[:, 8 + t:9 + t]),
                   after=("expert products", "yf in tokens", f"g{t} split"), mark=f"yf{t}")
                c.marks[free] = c.marks[f"yf{t}"]

            def load_residual(i, b):
                dma("sp", "res", lambda e: [e.dma_start(o[:, :, :], x_steps[i, b])], after=("store",))

            def add_attention(after=("res",), stored=None):
                op("dve", lambda e: e.reciprocal(rinv[:, :], rms[:, :]), after=("rms eps",), mark="rinv")
                for half in (0, 1):
                    bk, free = next_bank("energy")
                    op("pe", to_token_major(ya, bk, half), after=("ya0", "ya1", free), mark="ya in tokens")

                    def add(e):
                        for k in (0, 1):
                            n = 2 * half + k
                            last = e.scalar_tensor_tensor(o[:, n, :], bk[:, k * D:(k + 1) * D], rinv[:, n:n + 1],
                                                          o[:, n, :], ALU.mult, ALU.add)
                        return last
                    op("dve", add, after=("ya in tokens", "rinv") + after, mark="attention added")
                    if stored:
                        store(*stored, ("attention added",), slice(2 * half, 2 * half + 2))
                    c.marks[free] = c.marks["attention added"]

            def add_experts(after=("attention added",)):
                for half in (0, 1):
                    bk, free = next_bank("attention")
                    op("pe", to_token_major(yf, bk, half), after=("yf0", "yf1", free), mark="yf in tokens")
                    both = slice(2 * half, 2 * half + 2)
                    op("dve", lambda e: e.tensor_tensor(o[:, both, :].rearrange("p c d -> p (c d)"),
                                                        o[:, both, :].rearrange("p c d -> p (c d)"), bk[:, :],
                                                        ALU.add),
                       after=("yf in tokens",) + after, mark="experts added")
                    c.marks[free] = c.marks["experts added"]

            def store(i, b, after, chunks=slice(0, CH)):
                dma("sp", "store", lambda e: [e.dma_start(out_steps[i, b][:, chunks, :], o[:, chunks, :])], after=after)

            def to_token_major(src, bk, half):
                def go(e):
                    for k in (0, 1):
                        for t in range(KT):
                            tok = (2 * half + k) * P
                            last = e.transpose(bk[:, k * D + t * P:k * D + (t + 1) * P],
                                               src[:, t, tok:tok + P], ident[:, :])
                    return last
                return go

            def constants():
                op("pool", lambda e: e.memset(ident[:, :], 0.0), mark="ident 0")
                op("pool", lambda e: e.affine_select(out=ident[:, :], in_=ident[:, :], compare_op=ALU.not_equal,
                                                     fill=1.0, base=0, pattern=[[-1, P]], channel_multiplier=1),
                   after=("ident 0",), mark="ident")
                op("pool", lambda e: e.memset(causal[:, :], 0.5), mark="causal 0")
                op("pool", lambda e: e.affine_select(out=causal[:, :], in_=causal[:, :], compare_op=ALU.is_ge,
                                                     fill=0.0, base=0, pattern=[[1, P]],
                                                     channel_multiplier=-1),
                   after=("causal 0",), mark="causal")
                op("pool", lambda e: e.memset(expert_off[:, :, :], OFF), mark="expert_off 0")
                op("pool", lambda e: e.affine_select(out=expert_off[:, :, :], in_=expert_off[:, :, :],
                                                     compare_op=ALU.is_equal, fill=0.0, base=0,
                                                     pattern=[[-1, NE], [0, HE]], channel_multiplier=1),
                   after=("expert_off 0",), mark="expert_off")
                op("pool", lambda e: e.memset(half_pow[:, :], 0.5))
                op("pool", lambda e: e.memset(inv_half_pow[:, :], -0.5), mark="powers")

                def zeros(e):
                    for n in range(NE):
                        e.memset(rank[:, :, n:n + 1], float(NE - n))
                    for b in (0, 1):
                        e.memset(state[b][:, :], 0.0)
                        e.memset(off_T[b][:, :], 0.0)
                        e.memset(f32(on_T[b][:, :]), 0.0)
                    e.memset(f32(wg[:, :, :]), 0.0)
                    e.memset(onehot[:, :, :], 0.0)
                    return e.memset(f32(b2[:, :]), 0.0)
                op("dve", zeros, mark="zeros")
                op("dve", lambda e: e.memset(kv_bank[:, :], 0.0), mark="kv 0")
                for b in (0, 1):
                    c.marks[f"state{b}"] = c.marks["kv 0"]

            def load_weights():
                dma("act", "w_small", lambda e: [e.dma_start(cols[:, :], ins["cols"])]
                    + [e.dma_start(b2_raw[row:row + NE, :], ins["b2"]) for row in (0, NE_LO)], n=3)
                load_x(0, 0)
                for wi, what in enumerate("kvqu"):
                    dma("sp", f"w_{what}", lambda e, what=what, wi=wi: [e.dma_start(w_raw[what], ins["w_in"][wi])])
                load_x(0, 1)
                dma("sp", "w_1", lambda e: [e.dma_start(w1_raw.rearrange("p k n -> p (k n)"), ins["w_1"])])
                dma("sp", "w_2", lambda e: [e.dma_start(w2_raw, ins["w_2"])])
                dma("sp", "w_o", lambda e: [e.dma_start(wo_raw, ins["w_o"])])

            def small_weights():
                op("dve", lambda e: e.tensor_copy(wg[:, :, 0:NE], wg_cols), after=("zeros", "w_small"), mark="wg hi")
                for row in (0, NE_LO):
                    op("dve", lambda e, row=row: e.tensor_copy(b2[row:row + NE, :], b2_raw[row:row + NE, :]),
                       mark="b2 hi")
                op("dve", lambda e: e.tensor_tensor(wg[:, :, NE_LO:NE_LO + NE], wg_cols, f32(wg[:, :, 0:NE]),
                                                    ALU.subtract), after=("wg hi",), mark="wg")
                lo = slice(NE_LO, NE_LO + NE)
                op("dve", lambda e: e.tensor_tensor(b2[lo, :], b2_raw[lo, :], f32(b2[lo, :]), ALU.subtract),
                   after=("b2 hi",), mark="b2")

            def input_weight(what):
                wi = "kvqu".index(what)
                raw = w_raw[what].rearrange("p (k e) -> p k e", k=KT)
                split(w_hi[:, :, wi, :], w_lo[:, :, wi, :], raw, (f"w_{what}",), None, f"W{what}")

            def scale_w1():
                for k in range(KT):
                    op("pool", lambda e, k=k: e.tensor_tensor(
                        w1_sc[:, k, :].rearrange("p (x j) -> p x j", x=NE),
                        w1_raw[:, k, :].rearrange("p (x j) -> p x j", x=NE),
                        ln_cols[:, 0, k, :].unsqueeze(2).to_broadcast([P, NE, HE]), ALU.mult),
                       after=("w_small", "w_1", "Wk split", "Wv split"), mark="W1 scaled")

            def split_w1():
                for k in range(KT):
                    split(w1_hi[:, k, :], w1_lo[:, k, :], w1_sc[:, k, :], ("W1 scaled",), None, f"W1{k}", who="pool")

            def split_w2():
                split(w2_hi[:, :, :], w2_lo[:, :, :], w2_raw.rearrange("p (m d) -> p m d", m=MT), ("w_2",), None,
                      "W2", who="pool")

            def output_weight():
                for k in range(KT):
                    op("dve", lambda e, k=k: e.tensor_scalar(wo_sc[:, k * D:(k + 1) * D], wo_raw[:, k * D:(k + 1) * D],
                                                             vecs[:, 10 + k:11 + k], 0.5, ALU.mult, ALU.mult),
                       after=("w_o", "w_small"), mark="Wo scaled")
                split(wo_hi[:, :, :], wo_lo[:, :, :], wo_sc.rearrange("p (k e) -> p k e", k=KT),
                      ("Wo scaled",), None, "Wo", who="pool")

            def hidden_bias():
                bk, free = next_bank()

                def go(e):
                    for m in range(MT):
                        for k in range(KT):
                            last = e.matmul(bk[:, 2 * m:2 * m + 2], w1_raw[:, k, m * P:(m + 1) * P],
                                            ln_cols[:, 1, k, 2 * m:2 * m + 2], start=(k == 0), stop=(k == KT - 1))
                    return last
                op("pe", go, after=("w_small", "w_1", free), mark="ln_bias product")
                pairs = bk[:, 0:2 * MT].rearrange("p (m x) -> p m x", x=2)
                for x in (0, 1):
                    rows = slice(HE * x, HE * (x + 1))
                    op("dve", lambda e, x=x, rows=rows: e.tensor_tensor(
                        h_bias[rows, :], pairs[rows, :, x], vecs[rows, 12:16], ALU.add),
                       after=("ln_bias product",), mark="h_bias")
                c.marks[free] = c.marks["h_bias"]

            def tick(i, b, norm_next=True):
                n = 1 - b
                turn.clear()
                units = [(w, t) for w in "kvqu" for t in range(KT)]
                if norm_next:
                    load_x(i + 1, b)
                load_residual(i, b)
                for k in range(CH):
                    scores(b, k)
                    if k == 1 and norm_next:
                        norm_x(b)
                    if k == 3 and norm_next:
                        norm_again(b)
                    for w, t in units[2 * k:2 * k + 2]:
                        project(n, w, t)
                    attend(b, k)
                attention_out(b)
                spread_heads(n)
                gate_logits()
                hidden(b, 0)
                hidden(b, 1)
                if norm_next:
                    transpose_xn(0)
                    transpose_xn(1)
                hidden(b, 2)
                hidden(b, 3)
                op("act", lambda e: e.preload_act_table(ACT.Exp))
                choose_expert()
                split_keys(n)
                k_tokens(n, 0)
                k_tokens(n, 1)
                root_mean_square()
                attention_product(0)
                attention_product(1)
                v_tokens(n, 0)
                v_tokens(n, 1)
                gate_rows(n)
                expert_product(b, 0)
                expert_product(b, 1)
                add_attention()
                transpose_xh(n, 0)
                transpose_xh(n, 1)
                add_experts()
                store(i, b, ("experts added",))

            def last_tick(i, b):
                turn.clear()
                load_residual(i, b)
                for k in range(CH):
                    scores(b, k)
                    hidden(b, k, "dve")
                    attend(b, k)
                attention_out(b)
                expert_product(b, 0)
                expert_product(b, 1)
                root_mean_square()
                attention_product(0)
                add_experts(("res",))
                attention_product(1)
                add_attention(("experts added",), stored=(i, b))

            c.op("act", lambda e: e.preload_act_table(ACT.Exp))
            constants()
            load_weights()
            op("pool", lambda e: e.memset(f32(q_heads[0][:, :, :, :]), 0.0), mark="q_heads_hi 0")
            norm_x(0, "dve", meanwhile=lambda: input_weight("k"))
            op("act", lambda e: e.activation(q_heads[1][:, :, :, :].rearrange("p k h n -> p (k h) n"),
                                             f32(on_T[0][:, :]).unsqueeze(1).to_broadcast([P, KT * HPG, NT]),
                                             ACT.Copy), after=("zeros",), mark="q_heads_lo 0")
            transpose_xn(0)
            transpose_xn(1)
            split_w2()
            norm_again(0, meanwhile=lambda: input_weight("v"))
            norm_x(1)
            scale_w1()
            for what in "qu":
                input_weight(what)
            for w in "kvqu":
                for t in range(KT):
                    project(0, w, t, (f"W{w} split", "w_small"))
                if w == "k":
                    small_weights()
                if w == "v":
                    norm_again(1)
                if w == "q":
                    split_w1()
            gate_logits(("wg",))
            spread_heads(0, ("q_heads_hi 0", "q_heads_lo 0"))
            hidden_bias()
            k_tokens(0, 0)
            output_weight()
            k_tokens(0, 1)
            choose_expert()
            split_keys(0)
            v_tokens(0, 0)
            transpose_xh(0, 0)
            transpose_xn(0)
            transpose_xn(1)
            gate_rows(0)
            transpose_xh(0, 1)
            v_tokens(0, 1)

            pairs = STEPS // 2

            def body():
                tick(c.i if c.i is not None else 0, 0)
                tick(c.i if c.i is not None else 0, 1)
            c.loop(pairs - 1, body)
            tick(pairs - 1, 0, norm_next=False)
            last_tick(pairs - 1, 1)
            if c.me == "sp":
                c.wait("store")

        dry = Counts(None, None, sems)
        schedule(dry)
        body = dry.found

        block = ctx.enter_context(nc.Block())

        def run(me, eng):
            schedule(Counts(me, eng, sems, body, apart))

        @block.tensor
        def _(eng):
            run("pe", eng)

        @block.scalar
        def _(eng):
            run("act", eng)

        @block.vector
        def _(eng):
            run("dve", eng)

        @block.gpsimd
        def _(eng):
            run("pool", eng)

        @block.sync
        def _(eng):
            run("sp", eng)


def kernel(**inputs):
    import numpy as np
    import concourse.bacc as bacc
    from concourse.bass_utils import run_bass_kernel_spmd

    nc = bacc.Bacc("TRN2", target_bir_lowering=False, num_devices=1)
    a = {name.replace("L0_attn_", "").replace("L0_ffn_", ""): np.asarray(v) for name, v in inputs.items()}

    def by_feature(w):
        return w.T.reshape(KT, P, -1).transpose(1, 0, 2)

    vecs = np.concatenate([a[n].reshape(-1) for n in ("bk", "bv", "bq", "bu", "bo", "scale", "b1")]).reshape(16, P)
    laid = {
        "x": a["x"],
        "w_in": np.stack([by_feature(a[f"W{n}"]).reshape(P, -1) for n in "kvqu"]),
        "w_o": by_feature(a["Wo"]).reshape(P, -1),
        "w_1": by_feature(a["W1"].transpose(0, 2, 1).reshape(NE * HE, D)).reshape(P, -1),
        "w_2": a["W2"].reshape(MT, P, D).transpose(1, 0, 2).reshape(P, -1),
        "b2": a["b2"],
        "cols": np.concatenate([vecs.T] + [by_feature(a[n]).reshape(P, -1) for n in ("ln_scale", "ln_bias", "Wg")],
                               axis=1),
    }
    arrays, ins = {}, {}
    for name, value in laid.items():
        arrays[f"in_{name}"] = np.ascontiguousarray(value)
        ins[name] = nc.dram_tensor(f"in_{name}", value.shape, mybir.dt.from_np(value.dtype),
                                   kind="ExternalInput").ap()
    out = nc.dram_tensor("out", (B, T, D), F32, kind="ExternalOutput").ap()
    build(nc, ins, out)
    result = run_bass_kernel_spmd(nc, [arrays], core_ids=[0])
    return result.results[0]["out"]
```
